# Optimizing a Trainium2 kernel written in Bass

```python
import numpy as np
import jax
import jax.numpy as jnp

def _softmax(x, axis=-1):
    return jax.nn.softmax(x, axis=axis)

def _gelu(x):
    return jax.nn.gelu(x, approximate=True)

def _silu(x):
    return jax.nn.silu(x)

def _sigmoid(x):
    return jax.nn.sigmoid(x)

def _layernorm(x, axis=-1, eps=1e-05):
    m = jnp.mean(x, axis=axis, keepdims=True)
    v = jnp.var(x, axis=axis, keepdims=True)
    return (x - m) / jnp.sqrt(v + eps)

def _scatter_add(tgt, idx, src, axis=0):
    return tgt.at[idx].add(src)

def _segment_sum(src, seg, n):
    return jax.ops.segment_sum(src, seg, n)
kernel_name = 'mk_gnn_ffn_d1_gnn_r8_a0b4e6'

def setup_inputs(seed: int=0):
    np.random.seed(seed)
    _w = jnp.asarray

    def _rec_inputs():
        import jax
        import jax.numpy as jnp
        _gk = jax.random.key(seed)
        x = -0.0002117 + 1 * jax.random.normal(jax.random.fold_in(_gk, 1), (12500, 256), jnp.float32)
        src = jax.random.randint(jax.random.fold_in(_gk, 2), (200000,), 0, 12500, jnp.int32)
        dst = jax.random.randint(jax.random.fold_in(_gk, 3), (200000,), 0, 12500, jnp.int32)
        _o = jnp.argsort(dst, stable=True)
        src = src[_o]
        dst = dst[_o]
        return (x, src, dst)
    x, src, dst = _rec_inputs()

    def _L0_gnn_setup():
        import jax, jax.numpy as jnp
        import numpy as np
        N_NODES = 12500
        N_EDGES = 200000
        D_IN = 256
        D_OUT = 256
        key = jax.random.key(seed)
        k1, k2, k3, k4, k5 = jax.random.split(key, 5)
        feat = jax.random.normal(k1, (N_NODES, D_IN), dtype=jnp.float32)
        lim = float(np.sqrt(6.0 / (D_IN + D_OUT)))
        W_neigh = jax.random.uniform(k2, (D_OUT, D_IN), minval=-lim, maxval=lim, dtype=jnp.float32)
        W_self = jax.random.uniform(k3, (D_OUT, D_IN), minval=-lim, maxval=lim, dtype=jnp.float32)
        b_self = jnp.zeros((D_OUT,), dtype=jnp.float32)
        src = jax.random.randint(k4, (N_EDGES,), 0, N_NODES, dtype=jnp.int32)
        dst = jax.random.randint(k5, (N_EDGES,), 0, N_NODES, dtype=jnp.int32)
        return {'feat': feat, 'W_neigh': W_neigh, 'W_self': W_self, 'b_self': b_self, 'src': src, 'dst': dst}
    _L0_gnn_all = _L0_gnn_setup()
    _L0_gnn_in = {k: v for k, v in _L0_gnn_all.items() if k in ('W_neigh', 'W_self', 'b_self')}
    del _L0_gnn_all

    def _L0_ffn_setup():
        import math
        import jax, jax.numpy as jnp
        import numpy as np
        CAPACITY_FACTOR = 1.25
        TOP_K = 2
        LN_EPS = 1e-05

        def _layer_norm(x, gamma, beta):
            mu = jnp.mean(x, axis=-1, keepdims=True)
            var = jnp.var(x, axis=-1, keepdims=True)
            return (x - mu) * jax.lax.rsqrt(var + LN_EPS) * gamma + beta
        key = jax.random.key(seed)
        ks = jax.random.split(key, 4)
        B, S, D, F, E = (8, 512, 256, 512, 8)
        x = jax.random.normal(ks[0], (B, S, D), dtype=jnp.float32)
        Wr = jax.random.normal(ks[1], (D, E), dtype=jnp.float32) / np.sqrt(D)
        br = jnp.zeros((E,), jnp.float32)
        W1 = jax.random.normal(ks[2], (E, D, F), dtype=jnp.float32) / np.sqrt(D)
        b1 = jnp.zeros((E, F), jnp.float32)
        W2 = jax.random.normal(ks[3], (E, F, D), dtype=jnp.float32) / np.sqrt(F)
        b2 = jnp.zeros((E, D), jnp.float32)
        gamma = jnp.ones((D,), jnp.float32)
        beta = jnp.zeros((D,), jnp.float32)
        return {'x': x, 'Wr': Wr, 'br': br, 'W1': W1, 'b1': b1, 'W2': W2, 'b2': b2, 'gamma': gamma, 'beta': beta}
    _L0_ffn_all = _L0_ffn_setup()
    _L0_ffn_in = {k: v for k, v in _L0_ffn_all.items() if k in ('Wr', 'br', 'W1', 'b1', 'W2', 'b2', 'gamma', 'beta')}
    del _L0_ffn_all
    return {'x': x, 'src': src, 'dst': dst, 'L0_gnn_W_neigh': _L0_gnn_in['W_neigh'], 'L0_gnn_W_self': _L0_gnn_in['W_self'], 'L0_gnn_b_self': _L0_gnn_in['b_self'], 'L0_ffn_Wr': _L0_ffn_in['Wr'], 'L0_ffn_br': _L0_ffn_in['br'], 'L0_ffn_W1': _L0_ffn_in['W1'], 'L0_ffn_b1': _L0_ffn_in['b1'], 'L0_ffn_W2': _L0_ffn_in['W2'], 'L0_ffn_b2': _L0_ffn_in['b2'], 'L0_ffn_gamma': _L0_ffn_in['gamma'], 'L0_ffn_beta': _L0_ffn_in['beta']}

def reference(x, src, dst, L0_gnn_W_neigh, L0_gnn_W_self, L0_gnn_b_self, L0_ffn_Wr, L0_ffn_br, L0_ffn_W1, L0_ffn_b1, L0_ffn_W2, L0_ffn_b2, L0_ffn_gamma, L0_ffn_beta):
    import jax
    import jax.numpy as jnp

    def _L0_gnn_ref(feat, W_neigh, W_self, b_self, src, dst):
        import jax, jax.numpy as jnp
        import numpy as np
        N_NODES = 12500
        N_EDGES = 200000
        D_IN = 256
        D_OUT = 256
        msgs = feat[src]
        neigh_sum = jax.ops.segment_sum(msgs, dst, num_segments=N_NODES)
        deg = jax.ops.segment_sum(jnp.ones((src.shape[0],), dtype=feat.dtype), dst, num_segments=N_NODES)
        h_neigh = neigh_sum / jnp.maximum(deg, 1.0)[:, None]
        h_neigh = h_neigh @ W_neigh.T
        h_self = feat @ W_self.T + b_self
        return h_self + h_neigh

    def _L0_ffn_ref(x, Wr, br, W1, b1, W2, b2, gamma, beta):
        import math
        import jax, jax.numpy as jnp
        import numpy as np
        CAPACITY_FACTOR = 1.25
        TOP_K = 2
        LN_EPS = 1e-05

        def _layer_norm(x, gamma, beta):
            mu = jnp.mean(x, axis=-1, keepdims=True)
            var = jnp.var(x, axis=-1, keepdims=True)
            return (x - mu) * jax.lax.rsqrt(var + LN_EPS) * gamma + beta
        B, S, D = x.shape
        E = Wr.shape[1]
        N = B * S
        K = TOP_K
        logits = jnp.mean(x, axis=1) @ Wr + br
        routing_weights = jax.nn.softmax(logits, axis=-1)
        capacity = float(math.ceil(N * CAPACITY_FACTOR / E))
        expected_loads = routing_weights.sum(axis=0) * (N / B)
        scale = jnp.where(expected_loads > capacity, capacity / expected_loads, 1.0)
        routing_weights = jax.nn.softmax(routing_weights * scale, axis=-1)
        rw_tok = jnp.broadcast_to(routing_weights[:, None, :], (B, S, E)).reshape(N, E)
        top_w, top_i = jax.lax.top_k(rw_tok, K)
        top_w = jax.nn.softmax(top_w, axis=-1)
        xf = x.reshape(N, D)
        h = jax.nn.gelu(jnp.einsum('nd,edf->enf', xf, W1) + b1[:, None, :], approximate=False)
        y = jnp.einsum('enf,efd->end', h, W2) + b2[:, None, :]
        w_dense = jnp.zeros((N, E), x.dtype).at[jnp.arange(N)[:, None], top_i].add(top_w)
        out = jnp.einsum('ne,end->nd', w_dense, y).reshape(B, S, D)
        out = _layer_norm(out + x, gamma, beta)
        return out
    x = x + _L0_gnn_ref(_layernorm(x, axis=-1), L0_gnn_W_neigh, L0_gnn_W_self, L0_gnn_b_self, src, dst)
    x = x + _L0_ffn_ref(_layernorm(x, axis=-1)[None], L0_ffn_Wr, L0_ffn_br, L0_ffn_W1, L0_ffn_b1, L0_ffn_W2, L0_ffn_b2, L0_ffn_gamma, L0_ffn_beta)[0]
    return x

_drawn_inputs = setup_inputs


def setup_inputs(seed=0):
    import zlib

    import numpy as np

    out = dict(_drawn_inputs(seed))
    spreads = {'L0_gnn_b_self': (0.0, 0.1),
     'L0_ffn_br': (0.0, 0.1),
     'L0_ffn_b1': (0.0, 0.452),
     'L0_ffn_b2': (0.0, 0.304),
     'L0_ffn_gamma': (1.0, 0.2),
     'L0_ffn_beta': (0.0, 0.1)}
    factors = {}
    for name, (base, spread) in spreads.items():
        noise = np.random.default_rng([zlib.crc32(name.encode()), seed]).standard_normal(out[name].shape)
        drawn = base * np.exp(spread * noise) if base else spread * noise
        out[name] = jnp.asarray(drawn.astype(out[name].dtype))
    for name, factor in factors.items():
        out[name] = (out[name] * factor).astype(out[name].dtype)
    return out
```

```python
from contextlib import ExitStack

import concourse.bass as bass
import numpy as np
from concourse import mybir

P = 128
N_NODES = 12500
N_EDGES = 200000
D = 256
DC = D // P
EXPERTS = 8
HID = 512
HC = HID // P
TOP = 2
LN_EPS = 1e-5
CAPACITY = float(-(-(N_NODES * 5) // (4 * EXPERTS)))

NT = -(-N_NODES // P)
LAST_ROWS = N_NODES - (NT - 1) * P
NPAIR = NT // 2
ET = -(-N_EDGES // P)
ROUND = 32
CHUNK = 4
NCHUNK = ROUND // CHUNK
NROUND = -(-ET // ROUND)
ETP = NROUND * ROUND
EB = -(-ET // P)
MSGW = 2 * D + 2
NSEL = 2
PAD_DST = 1.0e6

S_ROW = 2048.0
S_W = 256.0
S_G = 16.0
S_PROD = S_ROW * S_W
S_B2 = 64.0

PREP_G = 7
PREP_T = NT // PREP_G
PREP_H = PREP_T // 2
FIN_T = 7
FIN_G = NT // FIN_T
FIN_B = 4


def gnn_ffn(nc, x, src, dst, w_neigh, w_self, b_self, wr, br, w1, b1, w2, b2, gamma, beta, out):
    f32, f16, i32 = mybir.dt.float32, mybir.dt.float16, mybir.dt.int32
    ALU, ACT, AX = mybir.AluOpType, mybir.ActivationFunctionType, mybir.AxisListType
    ds = bass.ds

    table = nc.dram_tensor("row_table", [NT * P, 2 * D], f16, kind="Internal").ap()
    ud = nc.dram_tensor("expert_out", [NT * P, 2 * D], f32, kind="Internal").ap()

    ctx = ExitStack()
    with ctx:
        def sb(name, shape, dt):
            return ctx.enter_context(nc.sbuf_tensor(name, shape, dt))

        def ps(name, shape, dt):
            return ctx.enter_context(nc.psum_tensor(name, shape, dt))

        def sem(name):
            return ctx.enter_context(nc.semaphore(name))

        X = sb("X", [P, NT, D], f32)
        src_t = sb("src_t", [P, ETP], i32)
        dst_t = sb("dst_t", [P, ETP], f32)
        idx_ring = sb("idx_ring", [P, 2, ROUND // 2], i32)
        sel = sb("sel", [P, NSEL * CHUNK * P], f16)
        window_n = sb("window_n", [P, P], f32)
        first_of = sb("first_of", [P, 1], f32)
        iota_n = sb("iota_n", [P, P], f16)
        iota_e = sb("iota_e", [1, EXPERTS], f32)
        ident = sb("ident", [P, P], f16)
        ident32 = sb("ident32", [P, P], f32)
        neg_base = sb("neg_base", [P, NT + 1], f32)
        ones = sb("ones", [P, P], f32)
        ones16 = sb("ones16", [1, 1], f16)
        zeros16 = sb("zeros16", [1, P], f16)
        stats = sb("stats", [P, PREP_T, 6], f32)
        mv = sb("mv", [P, NT, 2], f32)
        mv_pair = sb("mv_pair", [P, 2, 2], f32)
        rstd = sb("rstd", [P, NT], f32)
        nwt = sb("nwt", [P, 4, PREP_T], f32)
        gw = sb("gw", [P, 2, 2, DC, D], f16)
        bias_in = sb("bias_in", [1, TOP, D], f32)
        bias_lo = sb("bias_lo", [1, TOP, D], f16)
        bias_rows = sb("bias_rows", [2, 3, D], f16)
        bias_c = sb("bias_c", [2, 2, P], f16)
        gamma_b = sb("gamma_b", [P, D], f32)
        beta_b = sb("beta_b", [P, D], f32)
        te_row = sb("te_row", [1, NT + 1], i32)
        tab = sb("tab", [P, 2, 2 * D], f16)
        xT = sb("xT", [P, 2 * DC, P], f16)
        hn = sb("hn", [P, 2 * D], f16)
        hT = sb("hT", [P, 2 * DC, P], f16)
        rdeg = sb("rdeg", [P, 2, 2], f32)
        xs = sb("xs", [P, 2, D], f32)
        colsum = sb("colsum", [P, D], f32)
        x2 = sb("x2", [P, 2, 2 * D], f16)
        x2T = sb("x2T", [P, 2 * DC, 2 * P], f16)
        y1c = sb("y1c", [P, 2, D], f32)
        y_sb = sb("y_sb", [P, 2, 2 * D], f32)
        b1_t = sb("b1_t", [P, TOP, HC], f32)
        wr_t = sb("wr_t", [P, DC, EXPERTS], f32)
        rt = sb("rt", [1, 16, EXPERTS], f32)
        ri = sb("ri", [1, TOP], i32)
        mean_t = sb("mean_t", [P, DC], f32)
        wcol = sb("wcol", [P, 1], f32)
        MSG_F = ROUND * MSGW // 2
        W_F = TOP * 2 * DC * HID // 2
        G32_F, G16_F = 4 * 2 * P, TOP * HC * 2 * P // 2
        ARENA = MSG_F + 2 * W_F + G32_F + 2 * G16_F
        arena = sb("arena", [P, ARENA], f32)
        msg = arena[:, 0:MSG_F].bitcast(f16)
        o = MSG_F
        w1_s = arena[:, o:o + W_F].bitcast(f16).rearrange(
            "p (e a c h k) -> p e a c h k", e=TOP, a=2, c=DC, h=HC)
        o += W_F
        w2_s = arena[:, o:o + W_F].bitcast(f16).rearrange(
            "p (e a h n) -> p e a h n", e=TOP, a=2, h=HC)
        o += W_F
        g32 = arena[:, o:o + G32_F].rearrange("p (b h n) -> p b h n", b=2, h=2)
        w_stage = arena[:, o:o + G32_F]
        o += G32_F
        gh = arena[:, o:o + G16_F].bitcast(f16).rearrange("p (e h n) -> p e h n", e=TOP, h=HC)
        o += G16_F
        gl = arena[:, o:o + G16_F].bitcast(f16).rearrange("p (e h n) -> p e h n", e=TOP, h=HC)
        assert FIN_B * FIN_T * 2 * D <= ARENA
        fin = arena[:, 0:FIN_B * FIN_T * 2 * D].rearrange(
            "p (b t c) -> p b t c", b=FIN_B, t=FIN_T)
        IN_F = EB * P
        o = 0
        in_src = arena[:, o:o + IN_F].bitcast(i32).rearrange("p (b e) -> p b e", e=P)
        o += IN_F
        in_dst = arena[:, o:o + IN_F].bitcast(i32).rearrange("p (b e) -> p b e", e=P)
        o += IN_F
        in_f = arena[:, o:o + 2 * IN_F].rearrange("p (a b e) -> p a b e", a=2, e=P)
        o += 2 * IN_F
        below = arena[:, o:o + 2 * P].rearrange("p (a k) -> p a k", a=2)
        o += 2 * P
        xn = arena[:, o:o + PREP_T * D].rearrange("p (b c) -> p b c", b=PREP_T)
        o += PREP_T * D
        xw = arena[:, o:o + PREP_T * D].bitcast(f16).rearrange("p (b c) -> p b c", b=PREP_T)
        o += PREP_T * D
        w_in = arena[:, o:o + 4 * D].rearrange("p (a c f) -> p a c f", a=2, c=DC)
        assert o + 4 * D <= ARENA

        acc = ps("acc", [P, 512], f32)
        tp = [ps(f"tp{b}", [P, 2 * 2 * DC, P], f16) for b in range(2)]
        proj = ps("proj", [P, 512], f32)
        up = [ps(f"up{b}", [P, 2, 2 * P], f32) for b in range(2)]
        up_flat = [u[:, :, :].rearrange("p k n -> p (k n)") for u in up]
        yp = [ps(f"yp{b}", [P, TOP, D], f32) for b in range(2)]

        s_const = sem("s_const")
        s_pad = sem("s_pad")
        s_in = sem("s_in")
        s_small = sem("s_small")
        s_x = [sem(f"s_x{g}") for g in range(PREP_G)]
        s_dve = sem("s_dve")
        s_passed = sem("s_passed")
        s_cvt = sem("s_cvt")
        s_itp = sem("s_itp")
        s_icp = sem("s_icp")
        s_cmp = sem("s_cmp")
        s_cnt = sem("s_cnt")
        s_te = sem("s_te")
        s_wt = sem("s_wt")
        s_gw = sem("s_gw")
        s_xn = sem("s_xn")
        s_xhi = sem("s_xhi")
        s_xlo = sem("s_xlo")
        s_xst = [sem(f"s_xst{b}") for b in range(2)]
        s_idx = sem("s_idx")
        s_gather = [sem(f"s_gather{c}") for c in range(NCHUNK)]
        s_granted = sem("s_granted")
        s_msg = sem("s_msg")
        s_adv = sem("s_adv")
        s_sel = sem("s_sel")
        s_selfree = sem("s_selfree")
        s_tab = [sem(f"s_tab{b}") for b in range(2)]
        s_tx = sem("s_tx")
        s_xT = sem("s_xT")
        s_acc = sem("s_acc")
        s_rdeg = sem("s_rdeg")
        s_hhi = sem("s_hhi")
        s_hlo = sem("s_hlo")
        s_th = sem("s_th")
        s_hT = sem("s_hT")
        s_proj = sem("s_proj")
        s_pfree = sem("s_pfree")
        s_gnn = sem("s_gnn")
        s_mean = sem("s_mean")
        s_meanc = sem("s_meanc")
        s_log = sem("s_log")
        s_nmax = sem("s_nmax")
        s_exp = sem("s_exp")
        s_ridx = sem("s_ridx")
        s_w0 = sem("s_w0")
        s_wb = sem("s_wb")
        s_ebias = sem("s_ebias")
        s_wst = sem("s_wst")
        s_ew = sem("s_ew")
        s_blo = sem("s_blo")
        s_brow = sem("s_brow")
        s_x2s = sem("s_x2s")
        s_x2h = sem("s_x2h")
        s_x2l = sem("s_x2l")
        s_t2 = sem("s_t2")
        s_x2T = sem("s_x2T")
        s_up = sem("s_up")
        s_gelu = sem("s_gelu")
        s_gh = sem("s_gh")
        s_gl = sem("s_gl")
        s_y = sem("s_y")
        s_y1c = sem("s_y1c")
        s_yc = sem("s_yc")
        s_yfree = sem("s_yfree")
        s_yst = [sem(f"s_yst{b}") for b in range(2)]
        s_fl = [sem(f"s_fl{b}") for b in range(FIN_B)]
        s_fr = sem("s_fr")
        s_fn = sem("s_fn")
        s_fg = sem("s_fg")
        s_fo = sem("s_fo")
        s_fst = [sem(f"s_fst{b}") for b in range(FIN_B)]

        block = ctx.enter_context(nc.Block())

        x_rows = x[0:(NT - 1) * P, :].rearrange("(t p) f -> p t f", p=P)
        out_rows = out[0:(NT - 1) * P, :].rearrange("(t p) f -> p t f", p=P)
        ud_rows = ud.rearrange("(t p) f -> p t f", p=P)
        tab_rows = table.rearrange("(t p) f -> p t f", p=P)
        full_blocks = N_EDGES // (P * P)
        rest = N_EDGES - full_blocks * P * P
        rest_rows, rest_tail = rest // P, rest % P
        ADV_CREDIT = NCHUNK
        MSG_CREDIT = NCHUNK // 2 + 1

        class Order:

            def __init__(self, dve, base):
                self.dve, self.base, self.n = dve, base, 0

            def then(self, instruction):
                instruction.then_inc(s_dve, 1)
                self.n += 1
                self.dve.wait_ge(s_dve, self.base + self.n)

        @block.sync
        def _(sp):
            sp.wait_ge(s_pad, 3)
            for e, view in ((src, in_src), (dst, in_dst)):
                sp.dma_start(view[:, 0:full_blocks, :],
                             e[0:full_blocks * P * P].rearrange("(b t e) -> t b e", t=P, e=P)
                             ).then_inc(s_in, 16)
                at = full_blocks * P * P
                sp.dma_start(view[0:rest_rows, full_blocks, :],
                             e[at:at + rest_rows * P].rearrange("(t e) -> t e", e=P)
                             ).then_inc(s_in, 16)
                sp.dma_start(view[rest_rows:rest_rows + 1, full_blocks, 0:rest_tail],
                             e[at + rest_rows * P:N_EDGES].rearrange("(t e) -> t e", t=1)
                             ).then_inc(s_in, 16)
            for g in range(PREP_G):
                lo, hi = g * PREP_T, min((g + 1) * PREP_T, NT - 1)
                sp.dma_start(X[:, lo:hi, :], x_rows[:, lo:hi, :]).then_inc(s_x[g], 16)
            sp.dma_start(X[0:LAST_ROWS, NT - 1, :], x[(NT - 1) * P:N_NODES, :]
                         ).then_inc(s_x[PREP_G - 1], 16)
            sp.wait_ge(s_blo, 1)
            sp.dma_start(bias_rows[1:2, 0, :], bias_lo[0:1, 0, :]).then_inc(s_brow, 16)
            with sp.Fori(0, PREP_G) as g:
                for b in range(2):
                    sp.wait_ge(s_xlo, PREP_T * g + PREP_H * (b + 1))
                    sp.dma_start(tab_rows[:, ds(PREP_T * g + PREP_H * b, PREP_H), :],
                                 xw[:, PREP_H * b:PREP_H * (b + 1), :]).then_inc(s_xst[b], 16)

            sp.sem_inc(s_msg, MSG_CREDIT)
            with sp.Fori(0, NROUND) as i:
                for c in range(NCHUNK):
                    sp.wait_ge(s_gather[c], 16 * CHUNK * (i + 1))
                    sp.sem_inc(s_msg, 1)

            sp.wait_ge(s_ridx, 1)
            for e in range(TOP):
                idx = sp.value_load(ri[0:1, e:e + 1], min_val=0, max_val=EXPERTS - 1)
                sp.dma_start(b1_t[:, e, :], b1[ds(idx, 1), :].rearrange("a (p c) -> (a p) c", p=P)
                             ).then_inc(s_ebias, 16)
                sp.dma_start(bias_in[0:1, e, :], b2[ds(idx, 1), :]).then_inc(s_ebias, 16)
                if e:
                    sp.wait_ge(s_ew, 2 * e)
                sp.dma_start(w_stage.rearrange("p (c h) -> p c h", c=DC),
                             w1[ds(idx, 1), :, :].rearrange("a (c p) h -> p (a c) h", p=P)
                             ).then_inc(s_wst, 16)
                sp.wait_ge(s_ew, 2 * e + 1)
                sp.dma_start(w_stage.rearrange("p (c n) -> p c n", c=HC),
                             w2[ds(idx, 1), :, :].rearrange("a (p c) n -> p (a c) n", c=HC)
                             ).then_inc(s_wst, 16)
            sp.wait_ge(s_blo, 2)
            sp.dma_start(bias_rows[1:2, 1:3, :], bias_lo[0:1, :, :]).then_inc(s_brow, 16)
            with sp.Fori(0, NPAIR) as q:
                for h in range(2):
                    sp.wait_ge(s_yc, 2 * q + h + 3)
                    sp.dma_start(ud_rows[:, ds(2 * q + h, 1), :], y_sb[:, h:h + 1, :]
                                 ).then_inc(s_yst[h], 16)
                    sp.wait_ge(s_yst[h], 16 * (q + 1))
                    sp.sem_inc(s_yfree, 1)

            def load_group(g):
                sp.dma_start(fin[:, g % FIN_B, :, :], ud_rows[:, g * FIN_T:(g + 1) * FIN_T, :]
                             ).then_inc(s_fl[g % FIN_B], 16)

            for g in range(FIN_B - 1):
                load_group(g)
            for g in range(FIN_G):
                b = g % FIN_B
                ahead = g + FIN_B - 1
                if ahead < FIN_G:
                    if ahead >= FIN_B:
                        sp.wait_ge(s_fst[ahead % FIN_B], 16 * (ahead // FIN_B))
                    load_group(ahead)
                sp.wait_ge(s_fo, (g + 1) * FIN_T)
                lo, hi = g * FIN_T, min((g + 1) * FIN_T, NT - 1)
                sp.dma_start(out_rows[:, lo:hi, :], fin[:, b, 0:hi - lo, 0:D]).then_inc(s_fst[b], 16)
            b = (FIN_G - 1) % FIN_B
            sp.dma_start(out[(NT - 1) * P:N_NODES, :], fin[0:LAST_ROWS, b, FIN_T - 1, 0:D]
                         ).then_inc(s_fst[b], 16)
            for b in range(FIN_B):
                stores = len(range(b, FIN_G, FIN_B)) + (b == (FIN_G - 1) % FIN_B)
                sp.wait_ge(s_fst[b], 16 * stores)

        @block.gpsimd
        def _(pool):
            pool.memset(ident32[:, :], 0.0).then_inc(s_const, 1)
            pool.iota(neg_base[:, :], pattern=[[-P, NT + 1]], base=0, channel_multiplier=0,
                      allow_small_or_imprecise_dtypes=True).then_inc(s_const, 1)
            pool.iota(iota_n[:, :], pattern=[[1, P]], base=0, channel_multiplier=0,
                      allow_small_or_imprecise_dtypes=True).then_inc(s_const, 1)
            pool.iota(iota_e[:, :], pattern=[[1, EXPERTS]], base=0, channel_multiplier=0,
                      allow_small_or_imprecise_dtypes=True).then_inc(s_const, 1)
            pool.memset(ones[:, :], 1.0).then_inc(s_const, 1)
            pool.memset(ones16[:, :], 1.0).then_inc(s_const, 1)
            pool.memset(zeros16[:, :], 0.0).then_inc(s_const, 1)
            pool.memset(bias_c[:, 0, :], S_ROW).then_inc(s_const, 1)
            pool.memset(bias_c[:, 1, :], S_B2).then_inc(s_const, 1)
            pool.wait_ge(s_const, 9)
            pool.affine_select(out=ident32[:, :], in_=ident32[:, :], compare_op=ALU.not_equal,
                               fill=1.0, base=0, pattern=[[-1, P]], channel_multiplier=1
                               ).then_inc(s_const, 1)
            pool.wait_ge(s_const, 10)
            pool.tensor_copy(ident[:, :], ident32[:, :]).then_inc(s_const, 1)

            with pool.Fori(0, PREP_G) as g:
                for t in range(PREP_T):
                    pool.wait_ge(s_xhi, PREP_T * g + t + 1)
                    pool.tensor_tensor(out=xw[:, t, D:2 * D], in0=xn[:, t, :], in1=xw[:, t, 0:D],
                                       op=ALU.subtract).then_inc(s_xlo, 1)

            for b in range(2):
                pool.wait_ge(s_xst[b], 16 * PREP_G)
            pool.wait_ge(s_icp, 8)
            pool.wait_ge(s_te, 2)
            pool.wait_ge(s_gw, 2)
            pool.memset(msg.rearrange("p (s c) -> p s c", s=ROUND)[:, :, 2 * D:2 * D + 1], 1.0
                        ).then_inc(s_idx, 1)
            with pool.Fori(0, NROUND) as i:
                for half in range(2):
                    at = ROUND * i + half * (ROUND // 2)
                    pool.wait_ge(s_msg, NCHUNK * i + half * (NCHUNK // 2) + 1)
                    pool.sem_inc(s_granted, 1)
                    pool.tensor_copy(idx_ring[:, half, :], src_t[:, ds(at, ROUND // 2)]
                                     ).then_inc(s_idx, 1)
                    pool.wait_ge(s_idx, 2 * i + half + 2)
                    pool.sem_inc(s_granted, 1)
                    for c in range(NCHUNK // 2):
                        chunk = half * (NCHUNK // 2) + c
                        pool.wait_ge(s_adv, NCHUNK * i + chunk + 1)
                        pool.sem_inc(s_granted, 1)
                        for k in range(CHUNK):
                            s = chunk * CHUNK + k
                            col = s % (ROUND // 2)
                            pool.indirect_dma_start(
                                out=msg[:, s * MSGW:s * MSGW + 2 * D], out_offset=None,
                                in_=table[:, :],
                                in_offset=bass.IndirectOffsetOnAxis(
                                    ap=idx_ring[:, half, col:col + 1], axis=0),
                            ).then_inc(s_gather[chunk], 16)

            pool.wait_ge(s_small, 16 * 7)
            for g in range(FIN_G):
                for t in range(FIN_T):
                    pool.wait_ge(s_fn, g * FIN_T + t + 1)
                    tile = fin[:, g % FIN_B, t, D:2 * D]
                    pool.tensor_tensor(out=tile, in0=tile, in1=gamma_b[:, :], op=ALU.mult
                                       ).then_inc(s_fg, 1)

        @block.scalar
        def _(act):
            for a, w in enumerate((w_self, w_neigh)):
                act.dma_start(w_in[:, a, :, :], w.rearrange("(c p) f -> p c f", p=P)).then_inc(s_small, 16)
            act.dma_start(wr_t[:, :, :], wr.rearrange("(c p) e -> p c e", p=P)).then_inc(s_small, 16)
            act.dma_start(rt[0:1, 0, :], br.rearrange("(a e) -> a e", a=1)).then_inc(s_small, 16)
            act.dma_start(bias_in[0:1, 0, :], b_self.rearrange("(a f) -> a f", a=1)).then_inc(s_small, 16)
            act.dma_start(gamma_b[:, :], gamma.rearrange("(a f) -> a f", a=1).to_broadcast([P, D])
                          ).then_inc(s_small, 16)
            act.dma_start(beta_b[:, :], beta.rearrange("(a f) -> a f", a=1).to_broadcast([P, D])
                          ).then_inc(s_small, 16)

            n = 0
            for a, to in ((1, dst_t), (0, src_t)):
                for lo in range(0, EB, 4):
                    w = min(min(lo + 4, EB) * P, ETP) - lo * P
                    act.wait_ge(s_itp, n + 1)
                    act.activation(to[:, lo * P:lo * P + w], up_flat[n % 2][:, 0:w], ACT.Copy
                                   ).then_inc(s_icp, 1)
                    n += 1

            with act.Fori(0, PREP_G) as g:
                for t in range(PREP_T):
                    act.wait_ge(s_xn, PREP_T * g + t + 1)
                    act.activation(xw[:, t, 0:D], xn[:, t, :], ACT.Copy).then_inc(s_xhi, 1)

            def load_own(j, b):
                act.dma_start(tab[:, b, :], table[ds(j * P, P), :]).then_inc(s_tab[b], 16)

            for b in range(2):
                act.wait_ge(s_xst[b], 16 * PREP_G)
            load_own(0, 0)
            load_own(1, 1)

            def gnn_tile(j, b, load):
                act.wait_ge(s_tx, j + 1)
                act.activation(xT[:, :, :], tp[0][:, 0:2 * DC, :], ACT.Copy).then_inc(s_xT, 1)
                if load:
                    load_own(j + 2, b)
                act.wait_ge(s_acc, j + 1)
                act.wait_ge(s_rdeg, j + 1)
                act.activation(hn[:, 0:D], acc[:, 0:D], ACT.Copy, scale=rdeg[:, b, 1:2]
                               ).then_inc(s_hhi, 1)
                act.wait_ge(s_th, j + 1)
                act.activation(hT[:, :, :], tp[1][:, 0:2 * DC, :], ACT.Copy).then_inc(s_hT, 1)

            with act.Fori(0, NPAIR - 1) as p:
                for b in range(2):
                    gnn_tile(2 * p + b, b, True)
            for b in range(2):
                gnn_tile(NT - 2 + b, b, False)

            for k, (row, bias) in enumerate(((2, 3), (6, 7))):
                act.wait_ge(s_nmax, k + 1)
                act.activation(rt[0:1, row, :], rt[0:1, row, :], ACT.Exp, bias=rt[0:1, bias, 0:1],
                               accum_out=rt[0:1, bias, 1:2]).then_inc(s_exp, 1)
            act.wait_ge(s_nmax, 3)
            act.activation(rt[0:1, 10, 2:3], rt[0:1, 10, 1:2], ACT.Exp).then_inc(s_exp, 1)

            def expert_pair(q):
                for h in range(2):
                    act.wait_ge(s_x2s, 2 * q + h + 1)
                    act.activation(x2[:, h, 0:D], xs[:, h, :], ACT.Copy).then_inc(s_x2h, 1)
                for h in range(2):
                    act.wait_ge(s_t2, 2 * q + h + 1)
                    act.activation(x2T[:, :, h * P:(h + 1) * P], tp[h][:, 0:2 * DC, :], ACT.Copy
                                   ).then_inc(s_x2T, 1)
                for g in range(2 * TOP):
                    e, b = g // 2, g % 2
                    act.wait_ge(s_up, 4 * q + g + 1)
                    act.wait_ge(s_gl, 4 * q + g + 1)
                    for k in range(2):
                        last = act.activation(g32[:, b, k, :], up[b][:, k, :], ACT.Gelu,
                                              bias=b1_t[:, e, 2 * b + k:2 * b + k + 1],
                                              scale=1.0 / S_PROD)
                    last.then_inc(s_gelu, 1)
                    act.wait_ge(s_gelu, 4 * q + g + 3)
                    act.activation(gh[:, e, 2 * b:2 * b + 2, :], g32[:, b, :, :], ACT.Copy, scale=S_G
                                   ).then_inc(s_gh, 1)
                for h in range(2):
                    act.wait_ge(s_y, 2 * q + h + 1)
                    act.wait_ge(s_yc, 2 * q + h + 1)
                    act.activation(y1c[:, h, :], yp[h][:, 1, :], ACT.Copy, scale=S_ROW / (S_G * S_W)
                                   ).then_inc(s_y1c, 1)

            act.sem_inc(s_gelu, 2)
            act.wait_ge(s_ebias, 32 * TOP)
            act.wait_ge(s_ew, 2 * TOP)
            with act.Fori(0, NPAIR) as q:
                expert_pair(q)

            for g in range(FIN_G):
                act.wait_ge(s_fr, g + 1)
                for t in range(FIN_T):
                    j = g * FIN_T + t
                    act.activation(fin[:, g % FIN_B, t, D:2 * D], fin[:, g % FIN_B, t, 0:D],
                                   ACT.Identity, bias=mv[:, j, 0:1], scale=rstd[:, j:j + 1]
                                   ).then_inc(s_fn, 1)

        @block.tensor
        def _(pe):
            pe.sem_inc(s_adv, ADV_CREDIT)
            pe.sem_inc(s_selfree, NSEL)
            pe.wait_ge(s_const, 11)

            n = 0
            for a in (1, 0):
                pe.wait_ge(s_cvt, 1 if a else 2)
                for lo in range(0, EB, 4):
                    if n >= 2:
                        pe.wait_ge(s_icp, n - 1)
                    for k in range(lo, min(lo + 4, EB)):
                        last = pe.transpose(up_flat[n % 2][:, (k - lo) * P:(k - lo + 1) * P],
                                            in_f[:, a, k, :], ident32[:, :])
                    last.then_inc(s_itp, 1)
                    n += 1
            for k in range(EB):
                pe.wait_ge(s_cmp, k + 1)
                pe.matmul(proj[0:1, 0:NT], first_of[:, :], below[:, k % 2, 0:NT],
                          start=(k == 0), stop=(k == EB - 1)).then_inc(s_cnt, 1)
            pe.wait_ge(s_small, 16 * 7)
            for a in range(2):
                for ci in range(DC):
                    for co in range(DC):
                        last = pe.transpose(yp[a][:, ci, co * P:(co + 1) * P],
                                            w_in[:, a, co, ci * P:(ci + 1) * P], ident32[:, :])
                last.then_inc(s_wt, 1)
            pe.wait_ge(s_icp, 8)
            pe.wait_ge(s_gw, 2)
            pe.wait_ge(s_brow, 16)
            pe.wait_ge(s_te, 2)

            def split_product(to, left, right, more):
                k, last = 0, None
                for c in range(DC):
                    for i, j in ((0, 0), (0, 1), (1, 0)):
                        last = pe.matmul(to, left(i, c), right(j, c), start=False,
                                         stop=(not more and c == DC - 1 and (i, j) == (1, 0)))
                return last

            def window(j, b):
                first = pe.value_load(te_row[0:1, ds(j, 1)], min_val=1, max_val=NCHUNK * NROUND)
                end = pe.value_load(te_row[0:1, ds(j + 1, 1)], min_val=1, max_val=NCHUNK * NROUND)

                def step(c, start):
                    at = [pe.snap(((c + j) % NSEL) * (CHUNK * P) + k * P) for k in range(CHUNK)]
                    m = [pe.snap((c % NCHUNK) * (CHUNK * MSGW) + k * MSGW) for k in range(CHUNK)]
                    lo = [pe.snap((c % NCHUNK) * (CHUNK * MSGW) + k * MSGW + D) for k in range(CHUNK)]
                    pe.wait_ge(s_sel, c + j + 1)
                    pe.wait_ge(s_msg, c + 1 + MSG_CREDIT)
                    for k in range(CHUNK):
                        selector = sel[:, ds(at[k], P)]
                        low = pe.matmul(acc[:, 0:D + 1], selector, msg[:, ds(lo[k], D + 1)],
                                        start=start and k == 0, stop=False)
                        if not start and k == 0:
                            low.then_inc(s_adv, 1)
                        high = pe.matmul(acc[:, 0:D], selector, msg[:, ds(m[k], D)],
                                         start=False, stop=False)
                    high.then_inc(s_selfree, 1)

                step(first - 1, True)
                with pe.If(first < end):
                    with pe.Fori(first, end) as c:
                        step(c, False)
                pe.matmul(acc[:, 0:1], zeros16[0:1, :], ones16[0:1, 0:1], start=False, stop=True
                          ).then_inc(s_acc, 1)

            def gnn_tile(j, b, p):
                pe.wait_ge(s_tab[b], 16 * (p + 1))
                for k in range(2 * DC):
                    last = pe.transpose(tp[0][:, k, :], tab[:, b, k * P:(k + 1) * P], ident[:, :])
                last.then_inc(s_tx, 1)
                window(j, b)
                pe.wait_ge(s_hlo, j + 1)
                for k in range(2 * DC):
                    last = pe.transpose(tp[1][:, k, :], hn[:, k * P:(k + 1) * P], ident[:, :])
                last.then_inc(s_th, 1)
                pe.wait_ge(s_pfree, j + 1)
                pe.matmul(proj[:, 0:D], bias_c[0:2, 0, :], bias_rows[0:2, 0, :], start=True, stop=False)
                pe.wait_ge(s_xT, j + 1)
                split_product(proj[:, 0:D], lambda i, c: xT[:, i * DC + c, :],
                              lambda i, c: gw[:, 0, i, c, :], True)
                pe.wait_ge(s_hT, j + 1)
                split_product(proj[:, 0:D], lambda i, c: hT[:, i * DC + c, :],
                              lambda i, c: gw[:, 1, i, c, :], False).then_inc(s_proj, 1)

            with pe.Fori(0, NPAIR) as p:
                for b in range(2):
                    gnn_tile(2 * p + b, b, p)

            pe.wait_ge(s_gnn, 1)
            for c in range(DC):
                last = pe.matmul(proj[:, c:c + 1], colsum[:, c * P:(c + 1) * P], ones[:, 0:1],
                                 start=True, stop=True)
            last.then_inc(s_mean, 1)
            pe.wait_ge(s_meanc, 1)
            for c in range(DC):
                last = pe.matmul(proj[0:1, 16:16 + EXPERTS], mean_t[:, c:c + 1], wr_t[:, c, :],
                                 start=(c == 0), stop=(c == DC - 1))
            last.then_inc(s_log, 1)
            pe.wait_ge(s_w0, 1)
            pe.matmul(proj[:, 32:33], ones[0:1, :], rt[0:1, 11, 0:1], start=True, stop=True
                      ).then_inc(s_wb, 1)

            pe.wait_ge(s_ew, 2 * TOP)
            pe.wait_ge(s_brow, 32)

            def expert_pair(q):
                for h in range(2):
                    pe.wait_ge(s_x2l, 2 * q + h + 1)
                    for k in range(2 * DC):
                        last = pe.transpose(tp[h][:, k, :], x2[:, h, k * P:(k + 1) * P], ident[:, :])
                    last.then_inc(s_t2, 1)
                pe.wait_ge(s_x2T, 2 * q + 2)
                for g in range(2 * TOP):
                    e, b = g // 2, g % 2
                    pe.wait_ge(s_gelu, 4 * q + g + 1)
                    for k in range(2):
                        hc = 2 * b + k
                        for n, (c, i, j) in enumerate((c, i, j) for c in range(DC)
                                                      for i, j in ((0, 0), (0, 1), (1, 0))):
                            last = pe.matmul(up[b][:, k, :], w1_s[:, e, i, c, hc, :],
                                             x2T[:, j * DC + c, :], start=(n == 0),
                                             stop=(n == 3 * DC - 1))
                    last.then_inc(s_up, 1)
                for e in range(TOP):
                    pe.wait_ge(s_gl, 4 * q + 2 * e + 2 + 2)
                    for h in range(2):
                        if e == 0:
                            pe.wait_ge(s_yc, 2 * q + h + 1)
                        to = yp[h][:, e, :]
                        pe.matmul(to, bias_c[0:2, 1, :], bias_rows[0:2, 1 + e, :], start=True, stop=False)
                        for n, (hc, i, j) in enumerate((hc, i, j) for hc in range(HC)
                                                       for i, j in ((0, 0), (1, 0), (0, 1))):
                            g = (gh, gl)[i]
                            last = pe.matmul(to, g[:, e, hc, h * P:(h + 1) * P], w2_s[:, e, j, hc, :],
                                             start=False, stop=(n == 3 * HC - 1))
                        if e == TOP - 1:
                            last.then_inc(s_y, 1)

            with pe.Fori(0, NPAIR) as q:
                expert_pair(q)

        @block.vector
        def _(dve):
            dve.memset(X[:, NT - 1, :], 0.0).then_inc(s_pad, 1)
            dve.memset(in_src[:, full_blocks, :], 0).then_inc(s_pad, 1)
            dve.memset(in_dst[:, full_blocks, :], int(PAD_DST)).then_inc(s_pad, 1)
            dve.memset(colsum[:, :], 0.0)
            dve.memset(te_row[:, 0:1], 1).then_inc(s_te, 1)
            done = [0]

            dve.wait_ge(s_in, 16 * 6)
            dve.tensor_copy(in_f[:, 1, :, :], in_dst[:, :, :]).then_inc(s_cvt, 1)
            dve.tensor_copy(in_f[:, 0, :, :], in_src[:, :, :]).then_inc(s_cvt, 1)
            dve.wait_ge(s_cvt, 1)
            dve.wait_ge(s_const, 11)
            dve.reduce_sum(first_of[:, :], ident32[:, :].rearrange("p (c k) -> p k c", k=CHUNK)[:, 0, :], AX.X
                           ).then_inc(s_dve, 1)
            done[0] += 1
            dve.wait_ge(s_dve, done[0])
            for k in range(EB):
                if k >= 2:
                    dve.wait_ge(s_cnt, k - 1)
                dve.tensor_scalar(below[:, k % 2, 0:NT], neg_base[:, 1:NT + 1],
                                  in_f[:, 1, k, 0:1], 0.0, ALU.add, ALU.is_lt).then_inc(s_cmp, 1)
            dve.wait_ge(s_cnt, EB)
            dve.tensor_scalar_max(te_row[0:1, 1:NT + 1], proj[0:1, 0:NT], 1.0).then_inc(s_te, 1)

            for a in range(2):
                dve.wait_ge(s_wt, a + 1)
                dve.tensor_scalar(gw[:, a, 0, :, :], yp[a][:, :, :], S_W, None, ALU.mult
                                  ).then_inc(s_dve, 1)
                done[0] += 1
                dve.wait_ge(s_dve, done[0])
                dve.scalar_tensor_tensor(gw[:, a, 1, :, :], yp[a][:, :, :], S_W, gw[:, a, 0, :, :],
                                         ALU.mult, ALU.subtract).then_inc(s_gw, 1)
            dve.tensor_scalar(bias_rows[0:1, 0, :], bias_in[0:1, 0, :], S_W, None, ALU.mult
                              ).then_inc(s_dve, 1)
            done[0] += 1
            dve.wait_ge(s_dve, done[0])
            dve.scalar_tensor_tensor(bias_lo[0:1, 0, :], bias_in[0:1, 0, :], S_W,
                                     bias_rows[0:1, 0, :], ALU.mult, ALU.subtract).then_inc(s_blo, 1)

            def inverse_deviation(order, variance, to, n, scale, eps):
                v, y, a = nwt[:, 0, 0:n], nwt[:, 1, 0:n], nwt[:, 2, 0:n]
                order.then(dve.tensor_scalar(v, variance, scale, eps, ALU.mult, ALU.add))
                order.then(dve.tensor_scalar(y.bitcast(i32), v.bitcast(i32), -0.5, float(0x5F3759DF),
                                             ALU.mult, ALU.add))
                for k in range(3):
                    order.then(dve.scalar_tensor_tensor(a, y, -0.5, v, ALU.mult, ALU.mult))
                    order.then(dve.tensor_tensor(a, a, y, ALU.mult))
                    order.then(dve.scalar_tensor_tensor(to if k == 2 else y, a, 1.5, y,
                                                        ALU.add, ALU.mult))
            NEWTON = 11

            for g in range(PREP_G):
                dve.wait_ge(s_x[g], 16 if g < PREP_G - 1 else 32)
                with dve.Fori(0, PREP_T) as t:
                    dve.bn_stats(stats[:, ds(t, 1), :].rearrange("p a f -> p (a f)"),
                                 X[:, ds(t + g * PREP_T, 1), :].rearrange("p a f -> p (a f)")
                                 ).then_inc(s_dve, 1)
                done[0] += PREP_T
                dve.wait_ge(s_dve, done[0])
                for t in range(PREP_T):
                    dve.bn_aggr(mv[:, g * PREP_T + t, :], stats[:, t, :]).then_inc(s_dve, 1)
                done[0] += PREP_T
                dve.wait_ge(s_dve, done[0])
                order = Order(dve, done[0])
                inverse_deviation(order, mv[:, g * PREP_T:(g + 1) * PREP_T, 1],
                                  rstd[:, g * PREP_T:(g + 1) * PREP_T], PREP_T,
                                  S_ROW ** -2, LN_EPS * S_ROW ** -2)
                done[0] += order.n
                for b in range(2):
                    if g:
                        dve.wait_ge(s_xst[b], 16 * g)
                    for t in range(PREP_H * b, PREP_H * (b + 1)):
                        j = g * PREP_T + t
                        dve.tensor_scalar(xn[:, t, :], X[:, j, :], mv[:, j, 0:1], rstd[:, j:j + 1],
                                          ALU.subtract, ALU.mult).then_inc(s_xn, 1)

            dve.wait_ge(s_icp, 8)
            dve.wait_ge(s_te, 2)
            dve.sem_inc(s_pfree, 1)

            def window(order, j):
                first = dve.value_load(te_row[0:1, ds(j, 1)], min_val=1, max_val=NCHUNK * NROUND)
                end = dve.value_load(te_row[0:1, ds(j + 1, 1)], min_val=1, max_val=NCHUNK * NROUND)
                order.then(dve.tensor_scalar(window_n[:, :], iota_n[:, :], neg_base[:, ds(j, 1)], None,
                                             ALU.subtract))
                with dve.Fori(first - 1, end) as c:
                    dve.wait_ge(s_selfree, c + j + 1)
                    dve.tensor_tensor(
                        sel[:, ds(((c + j) % NSEL) * (CHUNK * P), CHUNK * P)
                            ].rearrange("p (k n) -> p k n", n=P),
                        window_n[:, :].rearrange("p (a n) -> p a n", a=1).to_broadcast([P, CHUNK, P]),
                        dst_t[:, ds(c * CHUNK, CHUNK)].rearrange("p (k a) -> p k a", a=1
                                                                 ).to_broadcast([P, CHUNK, P]),
                        ALU.is_equal).then_inc(s_sel, 1)

            def gnn_tile(order, j, b):
                dve.sem_inc(s_passed, 1)
                window(order, j)
                dve.wait_ge(s_acc, j + 1)
                order.then(dve.tensor_scalar_max(rdeg[:, b, 0:1], acc[:, D:D + 1], 1.0))
                dve.reciprocal(rdeg[:, b, 1:2], rdeg[:, b, 0:1]).then_inc(s_rdeg, 1)
                dve.wait_ge(s_rdeg, j + 1)
                dve.wait_ge(s_hhi, j + 1)
                dve.scalar_tensor_tensor(hn[:, D:2 * D], acc[:, 0:D], rdeg[:, b, 1:2], hn[:, 0:D],
                                         ALU.mult, ALU.subtract).then_inc(s_hlo, 1)
                dve.wait_ge(s_proj, j + 1)
                x1 = X[:, ds(j, 1), :].rearrange("p a f -> p (a f)")
                dve.scalar_tensor_tensor(x1, proj[:, 0:D], 1.0 / S_PROD, x1, ALU.mult, ALU.add
                                         ).then_inc(s_pfree, 1)
                dve.wait_ge(s_pfree, j + 2)
                dve.sem_inc(s_passed, 1)
                order.then(dve.bn_stats(stats[:, b, :], x1))
                dve.sem_inc(s_passed, 1)
                order.then(dve.bn_aggr(mv_pair[:, b, :], stats[:, b, :]))

            def normalise(j, b):
                return dve.tensor_scalar(xs[:, b, :], X[:, ds(j, 1), :].rearrange("p a f -> p (a f)"),
                                         mv[:, ds(j, 1), 0:1].rearrange("p a f -> p (a f)"),
                                         rstd[:, ds(j, 1)], ALU.subtract, ALU.mult)

            def gnn_pair(base, p, rows):
                order = Order(dve, base)
                for b in range(2):
                    gnn_tile(order, 2 * p + b, b)
                order.then(dve.tensor_copy(mv[:, ds(2 * p, 2), 0:1], mv_pair[:, :, 0:1]))
                inverse_deviation(order, mv_pair[:, :, 1],
                                  rstd[:, ds(2 * p, 2)], 2, S_ROW ** -2, LN_EPS * S_ROW ** -2)
                for b in range(2):
                    order.then(normalise(2 * p + b, b))
                for b in range(2):
                    r = rows[b]
                    order.then(dve.tensor_tensor(colsum[0:r, :], colsum[0:r, :], xs[0:r, b, :], ALU.add))
                return order.n
            PER_PAIR = 2 * 4 + 1 + NEWTON + 4
            base = done[0]
            with dve.Fori(0, NPAIR - 1) as p:
                assert gnn_pair(base + p * PER_PAIR, p, (P, P)) == PER_PAIR
            done[0] += (NPAIR - 1) * PER_PAIR
            done[0] += gnn_pair(done[0], NPAIR - 1, (P, LAST_ROWS))
            dve.sem_inc(s_gnn, 1)

            order = Order(dve, done[0])

            def row(k, n=EXPERTS, at=0):
                return rt[0:1, k, at:at + n]

            dve.wait_ge(s_mean, 1)
            dve.tensor_scalar(mean_t[:, :], proj[:, 0:DC], 1.0 / (S_ROW * N_NODES), None, ALU.mult
                              ).then_inc(s_meanc, 1)
            dve.wait_ge(s_log, 1)
            order.then(dve.tensor_tensor(row(2), proj[0:1, 16:16 + EXPERTS], row(0), ALU.add))

            def negative_max(k, of):
                order.then(dve.reduce_max(row(k, 1, 2), row(of), AX.X))
                dve.tensor_scalar(row(k, 1), row(k, 1, 2), -1.0, None, ALU.mult).then_inc(s_nmax, 1)

            negative_max(3, 2)
            dve.wait_ge(s_exp, 1)
            order.then(dve.reciprocal(row(3, 1, 3), row(3, 1, 1)))
            order.then(dve.tensor_scalar(row(4), row(2), row(3, 1, 3), None, ALU.mult))
            order.then(dve.tensor_scalar(row(5), row(4), float(N_NODES), None, ALU.mult))
            order.then(dve.reciprocal(row(9), row(5)))
            order.then(dve.tensor_scalar(row(9), row(9), CAPACITY, 1.0, ALU.mult, ALU.min))
            order.then(dve.tensor_tensor(row(6), row(4), row(9), ALU.mult))
            negative_max(7, 6)
            dve.wait_ge(s_exp, 2)
            order.then(dve.reciprocal(row(7, 1, 3), row(7, 1, 1)))
            order.then(dve.tensor_scalar(row(8), row(6), row(7, 1, 3), None, ALU.mult))
            for k in range(TOP):
                order.then(dve.reduce_max(row(12, 1, k), row(8), AX.X))
                order.then(dve.tensor_scalar(row(13), row(8), row(12, 1, k), 2.0 * EXPERTS,
                                             ALU.is_lt, ALU.mult))
                order.then(dve.tensor_tensor(row(13), row(13), iota_e[:, :], ALU.add))
                order.then(dve.tensor_reduce(row(14, 1, k), row(13), AX.X, ALU.min))
                if k == 0:
                    order.then(dve.tensor_scalar(row(15), iota_e[:, :], row(14, 1, 0), -2.0,
                                                 ALU.is_equal, ALU.mult))
                    order.then(dve.tensor_tensor(row(8), row(8), row(15), ALU.add))
            dve.tensor_copy(ri[:, :], row(14, TOP)).then_inc(s_ridx, 1)
            dve.tensor_tensor(row(10, 1, 1), row(12, 1, 1), row(12, 1, 0), ALU.subtract
                              ).then_inc(s_nmax, 1)
            dve.wait_ge(s_exp, 3)
            order.then(dve.tensor_scalar(row(10, 1, 3), row(10, 1, 2), 1.0, None, ALU.add))
            dve.reciprocal(row(11, 1), row(10, 1, 3)).then_inc(s_w0, 1)
            dve.wait_ge(s_wb, 1)
            order.then(dve.tensor_copy(wcol[:, :], proj[:, 32:33]))

            def split(hi, lo, view):
                order.then(dve.tensor_scalar(hi, view, S_W, None, ALU.mult))
                dve.scalar_tensor_tensor(lo, view, S_W, hi, ALU.mult, ALU.subtract).then_inc(s_ew, 1)

            for e in range(TOP):
                dve.wait_ge(s_wst, 32 * e + 16)
                for c in range(DC):
                    view = w_stage[:, c * HID:(c + 1) * HID].rearrange("p (k h) -> p h k", h=HC)
                    order.then(dve.tensor_scalar(w1_s[:, e, 0, c, :, :], view, S_W, None, ALU.mult))
                    low = dve.scalar_tensor_tensor(w1_s[:, e, 1, c, :, :], view, S_W,
                                                   w1_s[:, e, 0, c, :, :], ALU.mult, ALU.subtract)
                    if c == DC - 1:
                        low.then_inc(s_ew, 1)
                dve.wait_ge(s_wst, 32 * e + 32)
                split(w2_s[:, e, 0, :, :], w2_s[:, e, 1, :, :],
                      w_stage.rearrange("p (h n) -> p h n", h=HC))
            dve.wait_ge(s_ebias, 32 * TOP)
            order.then(dve.tensor_scalar(bias_rows[0:1, 1:3, :], bias_in[0:1, :, :], S_B2, None, ALU.mult))
            dve.scalar_tensor_tensor(bias_lo[0:1, :, :], bias_in[0:1, :, :], S_B2,
                                     bias_rows[0:1, 1:3, :], ALU.mult, ALU.subtract).then_inc(s_blo, 1)
            done[0] = order.base + order.n

            dve.sem_inc(s_gl, 2)
            dve.sem_inc(s_yc, 2)
            dve.sem_inc(s_yfree, 2)

            def expert_pair(base, q):
                order = Order(dve, base)
                for h in range(2):
                    normalise(2 * q + h, h).then_inc(s_x2s, 1)
                for h in range(2):
                    dve.wait_ge(s_x2h, 2 * q + h + 1)
                    dve.tensor_tensor(x2[:, h, D:2 * D], xs[:, h, :], x2[:, h, 0:D], ALU.subtract
                                      ).then_inc(s_x2l, 1)
                for g in range(2 * TOP):
                    e, b = g // 2, g % 2
                    dve.wait_ge(s_gh, 4 * q + g + 1)
                    dve.scalar_tensor_tensor(gl[:, e, 2 * b:2 * b + 2, :], g32[:, b, :, :], S_G,
                                             gh[:, e, 2 * b:2 * b + 2, :], ALU.mult, ALU.subtract
                                             ).then_inc(s_gl, 1)
                for h in range(2):
                    x1 = X[:, ds(2 * q + h, 1), :].rearrange("p a f -> p (a f)")
                    dve.tensor_tensor(x1, x1, beta_b[:, :], ALU.add).then_inc(s_dve, 1)
                for h in range(2):
                    dve.wait_ge(s_y, 2 * q + h + 1)
                    dve.wait_ge(s_yfree, 2 * q + h + 1)
                    dve.wait_ge(s_y1c, 2 * q + h + 1)
                    dve.tensor_tensor(y_sb[:, h, 0:D], xs[:, h, :], y1c[:, h, :], ALU.add
                                      ).then_inc(s_dve, 1)
                    dve.scalar_tensor_tensor(y_sb[:, h, D:2 * D], yp[h][:, 0, :], S_ROW / (S_G * S_W),
                                             y1c[:, h, :], ALU.mult, ALU.subtract).then_inc(s_yc, 1)
                dve.wait_ge(s_dve, base + 4)

            with dve.Fori(0, NPAIR) as q:
                expert_pair(done[0] + 4 * q, q)
            done[0] += 4 * NPAIR

            order = Order(dve, done[0])

            def outputs(g):
                for t in range(FIN_T):
                    j = g * FIN_T + t
                    dve.wait_ge(s_fg, j + 1)
                    dve.tensor_tensor(fin[:, g % FIN_B, t, 0:D], fin[:, g % FIN_B, t, D:2 * D],
                                      X[:, j, :], ALU.add).then_inc(s_fo, 1)

            for g in range(FIN_G):
                dve.wait_ge(s_fl[g % FIN_B], 16 * (g // FIN_B + 1))
                lo = g * FIN_T
                z = fin[:, g % FIN_B, :, 0:D]
                order.then(dve.scalar_tensor_tensor(z, fin[:, g % FIN_B, :, D:2 * D], wcol[:, :], z,
                                                    ALU.mult, ALU.add))
                for t in range(FIN_T):
                    dve.bn_stats(stats[:, t, :], fin[:, g % FIN_B, t, 0:D]).then_inc(s_dve, 1)
                order.n += FIN_T
                dve.wait_ge(s_dve, order.base + order.n)
                for t in range(FIN_T):
                    dve.bn_aggr(mv[:, lo + t, :], stats[:, t, :]).then_inc(s_dve, 1)
                order.n += FIN_T
                dve.wait_ge(s_dve, order.base + order.n)
                inverse_deviation(order, mv[:, lo:lo + FIN_T, 1], rstd[:, lo:lo + FIN_T], FIN_T,
                                  1.0, LN_EPS * S_ROW ** 2)
                dve.scalar_tensor_tensor(mv[:, lo:lo + FIN_T, 0], mv[:, lo:lo + FIN_T, 0], -1.0,
                                         rstd[:, lo:lo + FIN_T], ALU.mult, ALU.mult).then_inc(s_fr, 1)
                if g:
                    outputs(g - 1)
            outputs(FIN_G - 1)


INPUTS = ["x", "src", "dst", "L0_gnn_W_neigh", "L0_gnn_W_self", "L0_gnn_b_self", "L0_ffn_Wr", "L0_ffn_br",
          "L0_ffn_W1", "L0_ffn_b1", "L0_ffn_W2", "L0_ffn_b2", "L0_ffn_gamma", "L0_ffn_beta"]


def kernel(**inputs):
    import concourse.bacc as bacc
    from concourse.bass_utils import run_bass_kernel_spmd

    nc = bacc.Bacc("TRN2", target_bir_lowering=False, num_devices=1)
    arrays, args = {}, []
    for name in INPUTS:
        a = np.ascontiguousarray(inputs[name])
        arrays[f"in_{name}"] = a
        args.append(nc.dram_tensor(f"in_{name}", a.shape, mybir.dt.from_np(a.dtype),
                                   kind="ExternalInput").ap())
    args.append(nc.dram_tensor("out_0", (N_NODES, D), mybir.dt.float32, kind="ExternalOutput").ap())
    gnn_ffn(nc, *args)
    r = run_bass_kernel_spmd(nc, [arrays], core_ids=[0])
    return r.results[0]["out_0"]
```

```python
from contextlib import ExitStack

import concourse.bass as bass
import numpy as np
from concourse import mybir

P = 128
N_NODES = 12500
N_EDGES = 200000
D = 256
DC = D // P
EXPERTS = 8
HID = 512
HC = HID // P
TOP = 2
LN_EPS = 1e-5
CAPACITY = float(-(-(N_NODES * 5) // (4 * EXPERTS)))

NT = -(-N_NODES // P)
LAST_ROWS = N_NODES - (NT - 1) * P
NPAIR = NT // 2
ET = -(-N_EDGES // P)
ROUND = 32
CHUNK = 4
NCHUNK = ROUND // CHUNK
NROUND = -(-ET // ROUND)
ETP = NROUND * ROUND
EB = -(-ET // P)
MSGW = 2 * D + 2
NSEL = 2
PAD_DST = 1.0e6

S_ROW = 2048.0
S_W = 256.0
S_G = 16.0
S_PROD = S_ROW * S_W
S_B2 = 64.0

PREDICT = 6
LAG = PREDICT + 3

PREP_G = 7
PREP_T = NT // PREP_G
PREP_H = PREP_T // 2
FIN_T = 7
FIN_G = NT // FIN_T
FIN_B = 4


def gnn_ffn(nc, x, src, dst, w_neigh, w_self, b_self, wr, br, w1, b1, w2, b2, gamma, beta, out):
    f32, f16, i32 = mybir.dt.float32, mybir.dt.float16, mybir.dt.int32
    ALU, ACT, AX = mybir.AluOpType, mybir.ActivationFunctionType, mybir.AxisListType
    ds = bass.ds

    table = nc.dram_tensor("row_table", [NT * P, 2 * D], f16, kind="Internal").ap()
    ud = nc.dram_tensor("expert_out", [NT * P, 2 * D], f32, kind="Internal").ap()

    ctx = ExitStack()
    with ctx:
        def sb(name, shape, dt):
            return ctx.enter_context(nc.sbuf_tensor(name, shape, dt))

        def ps(name, shape, dt):
            return ctx.enter_context(nc.psum_tensor(name, shape, dt))

        def sem(name):
            return ctx.enter_context(nc.semaphore(name))

        X = sb("X", [P, NT, D], f32)
        src_t = sb("src_t", [P, ETP], i32)
        dst_t = sb("dst_t", [P, ETP], f32)
        idx_ring = sb("idx_ring", [P, 2, ROUND // 2], i32)
        sel = sb("sel", [P, NSEL * CHUNK * P], f16)
        window_n = sb("window_n", [P, P], f32)
        first_of = sb("first_of", [P, 1], f32)
        iota_n = sb("iota_n", [P, P], f16)
        iota_e = sb("iota_e", [1, EXPERTS], f32)
        ident = sb("ident", [P, P], f16)
        ident32 = sb("ident32", [P, P], f32)
        neg_base = sb("neg_base", [P, NT + 1], f32)
        ones = sb("ones", [P, P], f32)
        ones16 = sb("ones16", [1, 1], f16)
        zeros16 = sb("zeros16", [1, P], f16)
        stats = sb("stats", [P, PREP_T, 6], f32)
        mv = sb("mv", [P, NT, 2], f32)
        mv_pair = sb("mv_pair", [P, 2, 2], f32)
        rstd = sb("rstd", [P, NT], f32)
        nwt = sb("nwt", [P, 4, PREP_T], f32)
        gw = sb("gw", [P, 2, 2, DC, D], f16)
        bias_in = sb("bias_in", [1, TOP, D], f32)
        bias_lo = sb("bias_lo", [1, TOP, D], f16)
        bias_rows = sb("bias_rows", [2, 3, D], f16)
        bias_c = sb("bias_c", [2, 2, P], f16)
        gamma_b = sb("gamma_b", [P, D], f32)
        beta_b = sb("beta_b", [P, D], f32)
        te_row = sb("te_row", [1, NT + 1], i32)
        tab = sb("tab", [P, 2, 2 * D], f16)
        xT = sb("xT", [P, 2 * DC, P], f16)
        hn = sb("hn", [P, 2 * D], f16)
        hT = sb("hT", [P, 2 * DC, P], f16)
        rdeg = sb("rdeg", [P, 2, 2], f32)
        row_n = sb("row_n", [P, D], f32)
        xs = sb("xs", [P, 2, D], f32)
        colsum = sb("colsum", [P, D], f32)
        x2 = sb("x2", [P, 2, 2 * D], f16)
        x2T = sb("x2T", [P, 2 * DC, 2 * P], f16)
        y_sb = sb("y_sb", [P, 2, 2 * D], f32)
        b1_t = sb("b1_t", [P, TOP, HC], f32)
        wr_t = sb("wr_t", [P, DC, EXPERTS], f32)
        rt = sb("rt", [1, 20, EXPERTS], f32)
        ri = sb("ri", [1, 2, TOP + 1], i32)
        mean_t = sb("mean_t", [P, DC], f32)
        wcol = sb("wcol", [P, 1], f32)
        MSG_F = ROUND * MSGW // 2
        W_F = TOP * 2 * DC * HID // 2
        G32_F, G16_F = 4 * 2 * P, TOP * HC * 2 * P // 2
        ARENA = MSG_F + 2 * W_F + G32_F + 2 * G16_F
        arena = sb("arena", [P, ARENA], f32)
        msg = arena[:, 0:MSG_F].bitcast(f16)
        o = MSG_F
        w1_s = arena[:, o:o + W_F].bitcast(f16).rearrange(
            "p (e a c h k) -> p e a c h k", e=TOP, a=2, c=DC, h=HC)
        o += W_F
        w2_s = arena[:, o:o + W_F].bitcast(f16).rearrange(
            "p (e a h n) -> p e a h n", e=TOP, a=2, h=HC)
        o += W_F
        g32 = arena[:, o:o + G32_F].rearrange("p (b h n) -> p b h n", b=2, h=2)
        w_stage = (arena[:, o:o + G32_F], y_sb[:, :, :].rearrange("p a c -> p (a c)"))
        o += G32_F
        gh = arena[:, o:o + G16_F].bitcast(f16).rearrange("p (e h n) -> p e h n", e=TOP, h=HC)
        o += G16_F
        gl = arena[:, o:o + G16_F].bitcast(f16).rearrange("p (e h n) -> p e h n", e=TOP, h=HC)
        assert FIN_B * FIN_T * 2 * D <= ARENA
        fin = arena[:, 0:FIN_B * FIN_T * 2 * D].rearrange(
            "p (b t c) -> p b t c", b=FIN_B, t=FIN_T)
        IN_F = EB * P
        o = 0
        in_src = arena[:, o:o + IN_F].bitcast(i32).rearrange("p (b e) -> p b e", e=P)
        o += IN_F
        in_dst = arena[:, o:o + IN_F].bitcast(i32).rearrange("p (b e) -> p b e", e=P)
        o += IN_F
        in_f = arena[:, o:o + 2 * IN_F].rearrange("p (a b e) -> p a b e", a=2, e=P)
        o += 2 * IN_F
        below = arena[:, o:o + 2 * P].rearrange("p (a k) -> p a k", a=2)
        o += 2 * P
        xn = arena[:, o:o + PREP_T * D].rearrange("p (b c) -> p b c", b=PREP_T)
        o += PREP_T * D
        xw = arena[:, o:o + PREP_T * D].bitcast(f16).rearrange("p (b c) -> p b c", b=PREP_T)
        o += PREP_T * D
        w_in = arena[:, o:o + 4 * D].rearrange("p (a c f) -> p a c f", a=2, c=DC)
        assert o + 4 * D <= ARENA

        acc = ps("acc", [P, 512], f32)
        tp = [ps(f"tp{b}", [P, 2 * 2 * DC, P], f16) for b in range(2)]
        proj = ps("proj", [P, 512], f32)
        up = [ps(f"up{b}", [P, 2, 2 * P], f32) for b in range(2)]
        up_flat = [u[:, :, :].rearrange("p k n -> p (k n)") for u in up]
        up_16 = [u[:, 0:P * 2 * DC // 2].bitcast(f16).rearrange("p (k n) -> p k n", n=P)
                 for u in up_flat]
        yp = [ps(f"yp{b}", [P, TOP, D], f32) for b in range(2)]
        yp_flat = [y[:, :, :].rearrange("p e n -> p (e n)") for y in yp]

        s_const = sem("s_const")
        s_pad = sem("s_pad")
        s_in = sem("s_in")
        s_small = sem("s_small")
        s_x = [sem(f"s_x{g}") for g in range(PREP_G)]
        s_dve = sem("s_dve")
        s_dvf = sem("s_dvf")
        s_passed = sem("s_passed")
        s_cvt = sem("s_cvt")
        s_itp = sem("s_itp")
        s_icp = sem("s_icp")
        s_cmp = sem("s_cmp")
        s_cnt = sem("s_cnt")
        s_te = sem("s_te")
        s_wt = sem("s_wt")
        s_gw = sem("s_gw")
        s_xn = sem("s_xn")
        s_xhi = sem("s_xhi")
        s_xlo = sem("s_xlo")
        s_xst = [sem(f"s_xst{b}") for b in range(2)]
        s_idx = sem("s_idx")
        s_gather = [sem(f"s_gather{c}") for c in range(NCHUNK)]
        s_granted = sem("s_granted")
        s_msg = sem("s_msg")
        s_adv = sem("s_adv")
        s_sel = sem("s_sel")
        s_selfree = sem("s_selfree")
        s_tab = [sem(f"s_tab{b}") for b in range(2)]
        s_tx = sem("s_tx")
        s_xT = sem("s_xT")
        s_acc = sem("s_acc")
        s_rdeg = sem("s_rdeg")
        s_hhi = sem("s_hhi")
        s_hlo = sem("s_hlo")
        s_th = sem("s_th")
        s_hT = sem("s_hT")
        s_proj = sem("s_proj")
        s_pfree = sem("s_pfree")
        s_gnn = sem("s_gnn")
        s_mean = sem("s_mean")
        s_meanc = sem("s_meanc")
        s_log = sem("s_log")
        s_nmax = sem("s_nmax")
        s_exp = sem("s_exp")
        s_ridx = sem("s_ridx")
        s_w0 = sem("s_w0")
        s_wb = sem("s_wb")
        s_ebias = sem("s_ebias")
        s_wst = sem("s_wst")
        s_ew = sem("s_ew")
        s_blo = sem("s_blo")
        s_brow = sem("s_brow")
        s_x2s = sem("s_x2s")
        s_x2h = sem("s_x2h")
        s_x2l = sem("s_x2l")
        s_t2 = sem("s_t2")
        s_x2T = sem("s_x2T")
        s_up = sem("s_up")
        s_gelu = sem("s_gelu")
        s_gh = sem("s_gh")
        s_gl = sem("s_gl")
        s_y = sem("s_y")
        s_y1c = sem("s_y1c")
        s_yu = sem("s_yu")
        s_yc = sem("s_yc")
        s_yst = [sem(f"s_yst{b}") for b in range(2)]
        s_beta = sem("s_beta")
        s_fl = [sem(f"s_fl{b}") for b in range(FIN_B)]
        s_fr = sem("s_fr")
        s_fn = sem("s_fn")
        s_fg = sem("s_fg")
        s_fo = sem("s_fo")
        s_fst = [sem(f"s_fst{b}") for b in range(FIN_B)]

        block = ctx.enter_context(nc.Block())

        x_rows = x[0:(NT - 1) * P, :].rearrange("(t p) f -> p t f", p=P)
        out_rows = out[0:(NT - 1) * P, :].rearrange("(t p) f -> p t f", p=P)
        ud_rows = ud.rearrange("(t p) f -> p t f", p=P)
        tab_rows = table.rearrange("(t p) f -> p t f", p=P)
        full_blocks = N_EDGES // (P * P)
        rest = N_EDGES - full_blocks * P * P
        rest_rows, rest_tail = rest // P, rest % P
        ADV_CREDIT = NCHUNK
        MSG_CREDIT = NCHUNK // 2 + 1

        class Order:

            def __init__(self, dve, base, of=s_dve):
                self.dve, self.base, self.n, self.of = dve, base, 0, of

            def then(self, instruction):
                instruction.then_inc(self.of, 1)
                self.n += 1
                self.dve.wait_ge(self.of, self.base + self.n)

        @block.sync
        def _(sp):
            sp.wait_ge(s_pad, 3)
            for e, view in ((src, in_src), (dst, in_dst)):
                sp.dma_start(view[:, 0:full_blocks, :],
                             e[0:full_blocks * P * P].rearrange("(b t e) -> t b e", t=P, e=P)
                             ).then_inc(s_in, 16)
                at = full_blocks * P * P
                sp.dma_start(view[0:rest_rows, full_blocks, :],
                             e[at:at + rest_rows * P].rearrange("(t e) -> t e", e=P)
                             ).then_inc(s_in, 16)
                sp.dma_start(view[rest_rows:rest_rows + 1, full_blocks, 0:rest_tail],
                             e[at + rest_rows * P:N_EDGES].rearrange("(t e) -> t e", t=1)
                             ).then_inc(s_in, 16)
            for g in range(PREP_G):
                lo, hi = g * PREP_T, min((g + 1) * PREP_T, NT - 1)
                sp.dma_start(X[:, lo:hi, :], x_rows[:, lo:hi, :]).then_inc(s_x[g], 16)
            sp.dma_start(X[0:LAST_ROWS, NT - 1, :], x[(NT - 1) * P:N_NODES, :]
                         ).then_inc(s_x[PREP_G - 1], 16)
            sp.wait_ge(s_blo, 1)
            sp.dma_start(bias_rows[1:2, 0, :], bias_lo[0:1, 0, :]).then_inc(s_brow, 16)
            with sp.Fori(0, PREP_G) as g:
                for b in range(2):
                    sp.wait_ge(s_xlo, PREP_T * g + PREP_H * (b + 1))
                    sp.dma_start(tab_rows[:, ds(PREP_T * g + PREP_H * b, PREP_H), :],
                                 xw[:, PREP_H * b:PREP_H * (b + 1), :]).then_inc(s_xst[b], 16)

            sp.sem_inc(s_msg, MSG_CREDIT)
            with sp.Fori(0, NROUND) as i:
                for c in range(NCHUNK):
                    sp.wait_ge(s_gather[c], 16 * CHUNK * (i + 1))
                    sp.sem_inc(s_msg, 1)

            sp.wait_ge(s_ridx, 2)
            again = sp.value_load(ri[0:1, 1, TOP:TOP + 1], min_val=0, max_val=1)
            for h in range(2):
                sp.wait_ge(s_yst[h], again * (16 * NPAIR) + 16 * (NPAIR + 1))

            def load_group(g):
                sp.dma_start(fin[:, g % FIN_B, :, :], ud_rows[:, g * FIN_T:(g + 1) * FIN_T, :]
                             ).then_inc(s_fl[g % FIN_B], 16)

            for g in range(FIN_B - 1):
                load_group(g)
            for g in range(FIN_G):
                b = g % FIN_B
                ahead = g + FIN_B - 1
                if ahead < FIN_G:
                    if ahead >= FIN_B:
                        sp.wait_ge(s_fst[ahead % FIN_B], 16 * (ahead // FIN_B))
                    load_group(ahead)
                sp.wait_ge(s_fo, (g + 1) * FIN_T)
                lo, hi = g * FIN_T, min((g + 1) * FIN_T, NT - 1)
                sp.dma_start(out_rows[:, lo:hi, :], fin[:, b, 0:hi - lo, 0:D]).then_inc(s_fst[b], 16)
            b = (FIN_G - 1) % FIN_B
            sp.dma_start(out[(NT - 1) * P:N_NODES, :], fin[0:LAST_ROWS, b, FIN_T - 1, 0:D]
                         ).then_inc(s_fst[b], 16)
            for b in range(FIN_B):
                stores = len(range(b, FIN_G, FIN_B)) + (b == (FIN_G - 1) % FIN_B)
                sp.wait_ge(s_fst[b], 16 * stores)

        @block.gpsimd
        def _(pool):
            pool.memset(ident32[:, :], 0.0).then_inc(s_const, 1)
            pool.iota(neg_base[:, :], pattern=[[-P, NT + 1]], base=0, channel_multiplier=0,
                      allow_small_or_imprecise_dtypes=True).then_inc(s_const, 1)
            pool.iota(iota_n[:, :], pattern=[[1, P]], base=0, channel_multiplier=0,
                      allow_small_or_imprecise_dtypes=True).then_inc(s_const, 1)
            pool.iota(iota_e[:, :], pattern=[[1, EXPERTS]], base=0, channel_multiplier=0,
                      allow_small_or_imprecise_dtypes=True).then_inc(s_const, 1)
            pool.memset(ones[:, :], 1.0).then_inc(s_const, 1)
            pool.memset(ones16[:, :], 1.0).then_inc(s_const, 1)
            pool.memset(zeros16[:, :], 0.0).then_inc(s_const, 1)
            pool.memset(bias_c[:, 0, :], S_ROW).then_inc(s_const, 1)
            pool.memset(bias_c[:, 1, :], S_B2).then_inc(s_const, 1)
            pool.wait_ge(s_const, 9)
            pool.affine_select(out=ident32[:, :], in_=ident32[:, :], compare_op=ALU.not_equal,
                               fill=1.0, base=0, pattern=[[-1, P]], channel_multiplier=1
                               ).then_inc(s_const, 1)
            pool.wait_ge(s_const, 10)
            pool.tensor_copy(ident[:, :], ident32[:, :]).then_inc(s_const, 1)

            with pool.Fori(0, PREP_G) as g:
                for t in range(PREP_T):
                    pool.wait_ge(s_xhi, PREP_T * g + t + 1)
                    pool.tensor_tensor(out=xw[:, t, D:2 * D], in0=xn[:, t, :], in1=xw[:, t, 0:D],
                                       op=ALU.subtract).then_inc(s_xlo, 1)

            for b in range(2):
                pool.wait_ge(s_xst[b], 16 * PREP_G)
            pool.wait_ge(s_icp, 8)
            pool.wait_ge(s_te, 2)
            pool.wait_ge(s_gw, 2)
            pool.memset(msg.rearrange("p (s c) -> p s c", s=ROUND)[:, :, 2 * D:2 * D + 1], 1.0
                        ).then_inc(s_idx, 1)
            with pool.Fori(0, NROUND) as i:
                for half in range(2):
                    at = ROUND * i + half * (ROUND // 2)
                    pool.wait_ge(s_msg, NCHUNK * i + half * (NCHUNK // 2) + 1)
                    pool.sem_inc(s_granted, 1)
                    pool.tensor_copy(idx_ring[:, half, :], src_t[:, ds(at, ROUND // 2)]
                                     ).then_inc(s_idx, 1)
                    pool.wait_ge(s_idx, 2 * i + half + 2)
                    pool.sem_inc(s_granted, 1)
                    for c in range(NCHUNK // 2):
                        chunk = half * (NCHUNK // 2) + c
                        pool.wait_ge(s_adv, NCHUNK * i + chunk + 1)
                        pool.sem_inc(s_granted, 1)
                        for k in range(CHUNK):
                            s = chunk * CHUNK + k
                            col = s % (ROUND // 2)
                            pool.indirect_dma_start(
                                out=msg[:, s * MSGW:s * MSGW + 2 * D], out_offset=None,
                                in_=table[:, :],
                                in_offset=bass.IndirectOffsetOnAxis(
                                    ap=idx_ring[:, half, col:col + 1], axis=0),
                            ).then_inc(s_gather[chunk], 16)

            pool.wait_ge(s_small, 16 * 7)
            pool.wait_ge(s_ridx, 2)
            again = pool.value_load(ri[0:1, 1, TOP:TOP + 1], min_val=0, max_val=1)
            with pool.Fori(0, NT) as j:
                pool.wait_ge(s_x2s, again * NT + j + 1)
                pool.sem_inc(s_granted, 1)
                x1 = X[:, ds(j, 1), :].rearrange("p a f -> p (a f)")
                pool.tensor_tensor(out=x1, in0=x1, in1=beta_b[:, :], op=ALU.add).then_inc(s_beta, 1)

            for g in range(FIN_G):
                for t in range(FIN_T):
                    pool.wait_ge(s_fn, g * FIN_T + t + 1)
                    tile = fin[:, g % FIN_B, t, D:2 * D]
                    pool.tensor_tensor(out=tile, in0=tile, in1=gamma_b[:, :], op=ALU.mult
                                       ).then_inc(s_fg, 1)

        @block.scalar
        def _(act):
            for a, w in enumerate((w_self, w_neigh)):
                act.dma_start(w_in[:, a, :, :], w.rearrange("(c p) f -> p c f", p=P)).then_inc(s_small, 16)
            act.dma_start(wr_t[:, :, :], wr.rearrange("(c p) e -> p c e", p=P)).then_inc(s_small, 16)
            act.dma_start(rt[0:1, 0, :], br.rearrange("(a e) -> a e", a=1)).then_inc(s_small, 16)
            act.dma_start(bias_in[0:1, 0, :], b_self.rearrange("(a f) -> a f", a=1)).then_inc(s_small, 16)
            act.dma_start(gamma_b[:, :], gamma.rearrange("(a f) -> a f", a=1).to_broadcast([P, D])
                          ).then_inc(s_small, 16)
            act.dma_start(beta_b[:, :], beta.rearrange("(a f) -> a f", a=1).to_broadcast([P, D])
                          ).then_inc(s_small, 16)

            n = 0
            for a, to in ((1, dst_t), (0, src_t)):
                for lo in range(0, EB, 4):
                    w = min(min(lo + 4, EB) * P, ETP) - lo * P
                    act.wait_ge(s_itp, n + 1)
                    act.activation(to[:, lo * P:lo * P + w], up_flat[n % 2][:, 0:w], ACT.Copy
                                   ).then_inc(s_icp, 1)
                    n += 1

            with act.Fori(0, PREP_G) as g:
                for t in range(PREP_T):
                    act.wait_ge(s_xn, PREP_T * g + t + 1)
                    act.activation(xw[:, t, 0:D], xn[:, t, :], ACT.Copy).then_inc(s_xhi, 1)

            def load_own(j, b):
                act.dma_start(tab[:, b, :], table[ds(j * P, P), :]).then_inc(s_tab[b], 16)

            for b in range(2):
                act.wait_ge(s_xst[b], 16 * PREP_G)
            load_own(0, 0)
            load_own(1, 1)

            def own_rows(j, b, load):
                act.wait_ge(s_tx, j + 1)
                act.activation(xT[:, :, :], tp[0][:, 0:2 * DC, :], ACT.Copy).then_inc(s_xT, 1)
                if load:
                    load_own(j + 2, b)

            def mean_high(j, b):
                act.wait_ge(s_acc, j + 1)
                act.wait_ge(s_rdeg, j + 1)
                act.activation(hn[:, 0:D], acc[:, 0:D], ACT.Copy, scale=rdeg[:, b, 1:2]
                               ).then_inc(s_hhi, 1)

            def mean_copied(j):
                act.wait_ge(s_th, j + 1)
                act.activation(hT[:, :, :], tp[1][:, 0:2 * DC, :], ACT.Copy).then_inc(s_hT, 1)

            def rows_high(q):
                for h in range(2):
                    act.wait_ge(s_x2s, 2 * q + h + 1)
                    act.activation(x2[:, h, 0:D], xs[:, h, :], ACT.Copy).then_inc(s_x2h, 1)

            def rows_copied(q):
                for h in range(2):
                    act.wait_ge(s_t2, 2 * q + h + 1)
                    act.activation(x2T[:, :, h * P:(h + 1) * P], up_16[h], ACT.Copy
                                   ).then_inc(s_x2T, 1)

            def hidden(q, g):
                e, b = g // 2, g % 2
                act.wait_ge(s_up, 4 * q + g + 1)
                act.wait_ge(s_gl, 4 * q + g + 1)
                for k in range(2):
                    last = act.activation(g32[:, b, k, :], up[b][:, k, :], ACT.Gelu,
                                          bias=b1_t[:, e, 2 * b + k:2 * b + k + 1],
                                          scale=1.0 / S_PROD)
                last.then_inc(s_gelu, 1)
                act.wait_ge(s_gelu, 4 * q + g + 3)
                act.activation(gh[:, e, 2 * b:2 * b + 2, :], g32[:, b, :, :], ACT.Copy, scale=S_G
                               ).then_inc(s_gh, 1)

            def second_output(q):
                for h in range(2):
                    act.wait_ge(s_y, 2 * q + h + 1)
                    act.wait_ge(s_yst[h], 16 * (q + 1))
                    act.activation(y_sb[:, h, D:2 * D], yp[h][:, 1, :], ACT.Copy,
                                   scale=S_ROW / (S_G * S_W)).then_inc(s_y1c, 1)

            def store(q, tile):
                for h in range(2):
                    act.wait_ge(s_yc, 2 * q + h + 3)
                    act.dma_start(ud_rows[:, ds(tile + h, 1), :], y_sb[:, h:h + 1, :]
                                  ).then_inc(s_yst[h], 16)

            def expert_weights(k, e):
                idx = act.value_load(ri[0:1, k, e:e + 1], min_val=0, max_val=EXPERTS - 1)
                act.dma_start(b1_t[:, e, :], b1[ds(idx, 1), :].rearrange("a (p c) -> (a p) c", p=P)
                              ).then_inc(s_ebias, 16)
                act.dma_start(bias_in[0:1, e, :], b2[ds(idx, 1), :]).then_inc(s_ebias, 16)
                act.dma_start(w_stage[0].rearrange("p (c h) -> p c h", c=DC),
                              w1[ds(idx, 1), :, :].rearrange("a (c p) h -> p (a c) h", p=P)
                              ).then_inc(s_wst, 16)
                act.dma_start(w_stage[1].rearrange("p (c n) -> p c n", c=HC),
                              w2[ds(idx, 1), :, :].rearrange("a (p c) n -> p (a c) n", c=HC)
                              ).then_inc(s_wst, 16)

            def bias_low(k):
                act.wait_ge(s_blo, k + 2)
                act.dma_start(bias_rows[1:2, 1:3, :], bias_lo[0:1, :, :]).then_inc(s_brow, 16)

            def exponentials(k):
                for n, (row, bias) in enumerate(((2, 3), (6, 7))):
                    act.wait_ge(s_nmax, 2 * k + n + 1)
                    act.activation(rt[0:1, row, :], rt[0:1, row, :], ACT.Exp, bias=rt[0:1, bias, 0:1],
                                   accum_out=rt[0:1, bias, 1:2]).then_inc(s_exp, 1)

            def pair(p, q=None, between=None, ahead=False, load=True):
                j = 2 * p
                own_rows(j, 0, load)
                if q is not None:
                    rows_copied(q)
                if between:
                    between()
                mean_high(j, 0)
                if q is not None:
                    hidden(q, 0)
                    hidden(q, 1)
                mean_copied(j)
                if q is not None:
                    hidden(q, 2)
                own_rows(j + 1, 1, load)
                mean_high(j + 1, 1)
                if q is not None:
                    hidden(q, 3)
                mean_copied(j + 1)
                if q is not None:
                    second_output(q)
                if ahead:
                    rows_high(0 if q is None else q + 1)
                if q is not None:
                    store(q, 2 * q)

            def predicted():
                exponentials(0)
                act.wait_ge(s_ridx, 1)
                expert_weights(0, 0)

            def second_expert():
                act.wait_ge(s_ew, 2)
                expert_weights(0, 1)

            for h in range(2):
                act.sem_inc(s_yst[h], 16)
            act.sem_inc(s_gelu, 2)
            with act.Fori(0, PREDICT) as p:
                pair(p)
            pair(PREDICT, between=predicted)
            pair(PREDICT + 1, between=second_expert)
            pair(PREDICT + 2, between=lambda: bias_low(0), ahead=True)
            with act.Fori(LAG, NPAIR - 1) as p:
                pair(p, p - LAG, ahead=True)
            pair(NPAIR - 1, NPAIR - 1 - LAG, load=False)

            exponentials(1)
            act.wait_ge(s_nmax, 5)
            act.activation(rt[0:1, 10, 2:3], rt[0:1, 10, 1:2], ACT.Exp).then_inc(s_exp, 1)

            def experts_only(q, tile):
                rows_high(q)
                rows_copied(q)
                for g in range(2 * TOP):
                    hidden(q, g)
                second_output(q)
                store(q, tile)

            with act.Fori(NPAIR - LAG, NPAIR) as q:
                experts_only(q, 2 * q)
            again = act.value_load(ri[0:1, 1, TOP:TOP + 1], min_val=0, max_val=1)
            with act.If(again > 0):
                act.wait_ge(s_gl, 4 * NPAIR + 2)
                for h in range(2):
                    act.wait_ge(s_yst[h], 16 * (NPAIR + 1))
                expert_weights(1, 0)
                act.wait_ge(s_ew, 2 * TOP + 2)
                expert_weights(1, 1)
                bias_low(1)
                act.wait_ge(s_ebias, 64 * TOP)
                act.wait_ge(s_ew, 4 * TOP)
                with act.Fori(0, NPAIR) as q:
                    experts_only(q + NPAIR, 2 * q)

            for g in range(FIN_G):
                act.wait_ge(s_fr, g + 1)
                for t in range(FIN_T):
                    j = g * FIN_T + t
                    act.activation(fin[:, g % FIN_B, t, D:2 * D], fin[:, g % FIN_B, t, 0:D],
                                   ACT.Identity, bias=mv[:, j, 0:1], scale=rstd[:, j:j + 1]
                                   ).then_inc(s_fn, 1)

        @block.tensor
        def _(pe):
            pe.sem_inc(s_adv, ADV_CREDIT)
            pe.sem_inc(s_selfree, NSEL)
            pe.wait_ge(s_const, 11)

            n = 0
            for a in (1, 0):
                pe.wait_ge(s_cvt, 1 if a else 2)
                for lo in range(0, EB, 4):
                    if n >= 2:
                        pe.wait_ge(s_icp, n - 1)
                    for k in range(lo, min(lo + 4, EB)):
                        last = pe.transpose(up_flat[n % 2][:, (k - lo) * P:(k - lo + 1) * P],
                                            in_f[:, a, k, :], ident32[:, :])
                    last.then_inc(s_itp, 1)
                    n += 1
            for k in range(EB):
                pe.wait_ge(s_cmp, k + 1)
                pe.matmul(proj[0:1, 0:NT], first_of[:, :], below[:, k % 2, 0:NT],
                          start=(k == 0), stop=(k == EB - 1)).then_inc(s_cnt, 1)
            pe.wait_ge(s_small, 16 * 7)
            for a in range(2):
                for ci in range(DC):
                    for co in range(DC):
                        last = pe.transpose(yp[a][:, ci, co * P:(co + 1) * P],
                                            w_in[:, a, co, ci * P:(ci + 1) * P], ident32[:, :])
                last.then_inc(s_wt, 1)
            pe.wait_ge(s_icp, 8)
            pe.wait_ge(s_gw, 2)
            pe.wait_ge(s_brow, 16)
            pe.wait_ge(s_te, 2)

            def split_product(to, left, right, more):
                k, last = 0, None
                for c in range(DC):
                    for i, j in ((0, 0), (0, 1), (1, 0)):
                        last = pe.matmul(to, left(i, c), right(j, c), start=False,
                                         stop=(not more and c == DC - 1 and (i, j) == (1, 0)))
                return last

            def window(j, b):
                first = pe.value_load(te_row[0:1, ds(j, 1)], min_val=1, max_val=NCHUNK * NROUND)
                end = pe.value_load(te_row[0:1, ds(j + 1, 1)], min_val=1, max_val=NCHUNK * NROUND)

                def step(c, start):
                    at = [pe.snap(((c + j) % NSEL) * (CHUNK * P) + k * P) for k in range(CHUNK)]
                    m = [pe.snap((c % NCHUNK) * (CHUNK * MSGW) + k * MSGW) for k in range(CHUNK)]
                    lo = [pe.snap((c % NCHUNK) * (CHUNK * MSGW) + k * MSGW + D) for k in range(CHUNK)]
                    pe.wait_ge(s_sel, c + j + 1)
                    pe.wait_ge(s_msg, c + 1 + MSG_CREDIT)
                    for k in range(CHUNK):
                        selector = sel[:, ds(at[k], P)]
                        low = pe.matmul(acc[:, 0:D + 1], selector, msg[:, ds(lo[k], D + 1)],
                                        start=start and k == 0, stop=False)
                        if not start and k == 0:
                            low.then_inc(s_adv, 1)
                        high = pe.matmul(acc[:, 0:D], selector, msg[:, ds(m[k], D)],
                                         start=False, stop=False)
                    high.then_inc(s_selfree, 1)

                step(first - 1, True)
                with pe.If(first < end):
                    with pe.Fori(first, end) as c:
                        step(c, False)
                pe.matmul(acc[:, 0:1], zeros16[0:1, :], ones16[0:1, 0:1], start=False, stop=True
                          ).then_inc(s_acc, 1)

            def own_rows(j, b, p):
                pe.wait_ge(s_tab[b], 16 * (p + 1))
                for k in range(2 * DC):
                    last = pe.transpose(tp[0][:, k, :], tab[:, b, k * P:(k + 1) * P], ident[:, :])
                last.then_inc(s_tx, 1)

            def means(j):
                pe.wait_ge(s_hlo, j + 1)
                for k in range(2 * DC):
                    last = pe.transpose(tp[1][:, k, :], hn[:, k * P:(k + 1) * P], ident[:, :])
                last.then_inc(s_th, 1)

            def projection(j):
                pe.wait_ge(s_pfree, j + 1)
                pe.matmul(proj[:, 0:D], bias_c[0:2, 0, :], bias_rows[0:2, 0, :], start=True, stop=False)
                pe.wait_ge(s_xT, j + 1)
                split_product(proj[:, 0:D], lambda i, c: xT[:, i * DC + c, :],
                              lambda i, c: gw[:, 0, i, c, :], True)
                pe.wait_ge(s_hT, j + 1)
                split_product(proj[:, 0:D], lambda i, c: hT[:, i * DC + c, :],
                              lambda i, c: gw[:, 1, i, c, :], False).then_inc(s_proj, 1)

            def rows_transposed(q):
                pe.wait_ge(s_gelu, 4 * q + 2)
                for h in range(2):
                    pe.wait_ge(s_x2l, 2 * q + h + 1)
                    for k in range(2 * DC):
                        last = pe.transpose(up_16[h][:, k, :], x2[:, h, k * P:(k + 1) * P], ident[:, :])
                    last.then_inc(s_t2, 1)
                pe.wait_ge(s_x2T, 2 * q + 2)

            def hidden(q, g):
                e, b = g // 2, g % 2
                pe.wait_ge(s_gelu, 4 * q + g + 1)
                for k in range(2):
                    hc = 2 * b + k
                    for n, (c, i, j) in enumerate((c, i, j) for c in range(DC)
                                                  for i, j in ((0, 0), (0, 1), (1, 0))):
                        last = pe.matmul(up[b][:, k, :], w1_s[:, e, i, c, hc, :],
                                         x2T[:, j * DC + c, :], start=(n == 0),
                                         stop=(n == 3 * DC - 1))
                last.then_inc(s_up, 1)

            def outputs(q, e):
                pe.wait_ge(s_gl, 4 * q + 2 * e + 2 + 2)
                for h in range(2):
                    if e == 0:
                        pe.wait_ge(s_yc, 2 * q + h + 1)
                    to = yp[h][:, e, :]
                    pe.matmul(to, bias_c[0:2, 1, :], bias_rows[0:2, 1 + e, :], start=True, stop=False)
                    for n, (hc, i, j) in enumerate((hc, i, j) for hc in range(HC)
                                                   for i, j in ((0, 0), (1, 0), (0, 1))):
                        g = (gh, gl)[i]
                        last = pe.matmul(to, g[:, e, hc, h * P:(h + 1) * P], w2_s[:, e, j, hc, :],
                                         start=False, stop=(n == 3 * HC - 1))
                    if e == TOP - 1:
                        last.then_inc(s_y, 1)

            def router(k, bank):
                pe.wait_ge(s_gnn, k + 1)
                for c in range(DC):
                    last = pe.matmul(bank[:, c:c + 1], colsum[:, c * P:(c + 1) * P], ones[:, 0:1],
                                     start=True, stop=True)
                last.then_inc(s_mean, 1)
                pe.wait_ge(s_meanc, k + 1)
                for c in range(DC):
                    last = pe.matmul(bank[0:1, 16:16 + EXPERTS], mean_t[:, c:c + 1], wr_t[:, c, :],
                                     start=(c == 0), stop=(c == DC - 1))
                last.then_inc(s_log, 1)

            def pair(p, q=None, between=None):
                j = 2 * p
                own_rows(j, 0, p)
                window(j, 0)
                if between:
                    between()
                if q is not None:
                    rows_transposed(q)
                    hidden(q, 0)
                    hidden(q, 1)
                means(j)
                if q is not None:
                    hidden(q, 2)
                projection(j)
                own_rows(j + 1, 1, p)
                window(j + 1, 1)
                if q is not None:
                    hidden(q, 3)
                    outputs(q, 0)
                means(j + 1)
                if q is not None:
                    outputs(q, 1)
                projection(j + 1)

            with pe.Fori(0, PREDICT) as p:
                pair(p)
            pair(PREDICT, between=lambda: router(0, yp_flat[0]))
            pair(PREDICT + 1)
            pair(PREDICT + 2)
            pe.wait_ge(s_ew, 2 * TOP)
            pe.wait_ge(s_brow, 32)
            with pe.Fori(LAG, NPAIR) as p:
                pair(p, p - LAG)

            router(1, proj)
            pe.wait_ge(s_w0, 1)
            pe.matmul(proj[:, 32:33], ones[0:1, :], rt[0:1, 11, 0:1], start=True, stop=True
                      ).then_inc(s_wb, 1)

            def experts_only(q):
                rows_transposed(q)
                for g in range(2 * TOP):
                    hidden(q, g)
                for e in range(TOP):
                    outputs(q, e)

            with pe.Fori(NPAIR - LAG, NPAIR) as q:
                experts_only(q)
            again = pe.value_load(ri[0:1, 1, TOP:TOP + 1], min_val=0, max_val=1)
            with pe.If(again > 0):
                pe.wait_ge(s_ew, 4 * TOP)
                pe.wait_ge(s_brow, 48)
                with pe.Fori(NPAIR, 2 * NPAIR) as q:
                    experts_only(q)

        @block.vector
        def _(dve):
            dve.memset(X[:, NT - 1, :], 0.0).then_inc(s_pad, 1)
            dve.memset(in_src[:, full_blocks, :], 0).then_inc(s_pad, 1)
            dve.memset(in_dst[:, full_blocks, :], int(PAD_DST)).then_inc(s_pad, 1)
            dve.memset(colsum[:, :], 0.0)
            dve.memset(te_row[:, 0:1], 1).then_inc(s_te, 1)
            done = [0]

            dve.wait_ge(s_in, 16 * 6)
            dve.tensor_copy(in_f[:, 1, :, :], in_dst[:, :, :]).then_inc(s_cvt, 1)
            dve.tensor_copy(in_f[:, 0, :, :], in_src[:, :, :]).then_inc(s_cvt, 1)
            dve.wait_ge(s_cvt, 1)
            dve.wait_ge(s_const, 11)
            dve.reduce_sum(first_of[:, :], ident32[:, :].rearrange("p (c k) -> p k c", k=CHUNK)[:, 0, :], AX.X
                           ).then_inc(s_dve, 1)
            done[0] += 1
            dve.wait_ge(s_dve, done[0])
            for k in range(EB):
                if k >= 2:
                    dve.wait_ge(s_cnt, k - 1)
                dve.tensor_scalar(below[:, k % 2, 0:NT], neg_base[:, 1:NT + 1],
                                  in_f[:, 1, k, 0:1], 0.0, ALU.add, ALU.is_lt).then_inc(s_cmp, 1)
            dve.wait_ge(s_cnt, EB)
            dve.tensor_scalar_max(te_row[0:1, 1:NT + 1], proj[0:1, 0:NT], 1.0).then_inc(s_te, 1)

            for a in range(2):
                dve.wait_ge(s_wt, a + 1)
                dve.tensor_scalar(gw[:, a, 0, :, :], yp[a][:, :, :], S_W, None, ALU.mult
                                  ).then_inc(s_dve, 1)
                done[0] += 1
                dve.wait_ge(s_dve, done[0])
                dve.scalar_tensor_tensor(gw[:, a, 1, :, :], yp[a][:, :, :], S_W, gw[:, a, 0, :, :],
                                         ALU.mult, ALU.subtract).then_inc(s_gw, 1)
            dve.tensor_scalar(bias_rows[0:1, 0, :], bias_in[0:1, 0, :], S_W, None, ALU.mult
                              ).then_inc(s_dve, 1)
            done[0] += 1
            dve.wait_ge(s_dve, done[0])
            dve.scalar_tensor_tensor(bias_lo[0:1, 0, :], bias_in[0:1, 0, :], S_W,
                                     bias_rows[0:1, 0, :], ALU.mult, ALU.subtract).then_inc(s_blo, 1)

            def inverse_deviation(order, variance, to, n, scale, eps):
                v, y, a = nwt[:, 0, 0:n], nwt[:, 1, 0:n], nwt[:, 2, 0:n]
                order.then(dve.tensor_scalar(v, variance, scale, eps, ALU.mult, ALU.add))
                order.then(dve.tensor_scalar(y.bitcast(i32), v.bitcast(i32), -0.5, float(0x5F3759DF),
                                             ALU.mult, ALU.add))
                for k in range(3):
                    order.then(dve.scalar_tensor_tensor(a, y, -0.5, v, ALU.mult, ALU.mult))
                    order.then(dve.tensor_tensor(a, a, y, ALU.mult))
                    order.then(dve.scalar_tensor_tensor(to if k == 2 else y, a, 1.5, y,
                                                        ALU.add, ALU.mult))
            NEWTON = 11

            for g in range(PREP_G):
                dve.wait_ge(s_x[g], 16 if g < PREP_G - 1 else 32)
                with dve.Fori(0, PREP_T) as t:
                    dve.bn_stats(stats[:, ds(t, 1), :].rearrange("p a f -> p (a f)"),
                                 X[:, ds(t + g * PREP_T, 1), :].rearrange("p a f -> p (a f)")
                                 ).then_inc(s_dve, 1)
                done[0] += PREP_T
                dve.wait_ge(s_dve, done[0])
                for t in range(PREP_T):
                    dve.bn_aggr(mv[:, g * PREP_T + t, :], stats[:, t, :]).then_inc(s_dve, 1)
                done[0] += PREP_T
                dve.wait_ge(s_dve, done[0])
                order = Order(dve, done[0])
                inverse_deviation(order, mv[:, g * PREP_T:(g + 1) * PREP_T, 1],
                                  rstd[:, g * PREP_T:(g + 1) * PREP_T], PREP_T,
                                  S_ROW ** -2, LN_EPS * S_ROW ** -2)
                done[0] += order.n
                for b in range(2):
                    if g:
                        dve.wait_ge(s_xst[b], 16 * g)
                    for t in range(PREP_H * b, PREP_H * (b + 1)):
                        j = g * PREP_T + t
                        dve.tensor_scalar(xn[:, t, :], X[:, j, :], mv[:, j, 0:1], rstd[:, j:j + 1],
                                          ALU.subtract, ALU.mult).then_inc(s_xn, 1)

            dve.wait_ge(s_icp, 8)
            dve.wait_ge(s_te, 2)
            dve.sem_inc(s_pfree, 1)

            def window(order, j):
                first = dve.value_load(te_row[0:1, ds(j, 1)], min_val=1, max_val=NCHUNK * NROUND)
                end = dve.value_load(te_row[0:1, ds(j + 1, 1)], min_val=1, max_val=NCHUNK * NROUND)
                order.then(dve.tensor_scalar(window_n[:, :], iota_n[:, :], neg_base[:, ds(j, 1)], None,
                                             ALU.subtract))
                with dve.Fori(first - 1, end) as c:
                    dve.wait_ge(s_selfree, c + j + 1)
                    dve.tensor_tensor(
                        sel[:, ds(((c + j) % NSEL) * (CHUNK * P), CHUNK * P)
                            ].rearrange("p (k n) -> p k n", n=P),
                        window_n[:, :].rearrange("p (a n) -> p a n", a=1).to_broadcast([P, CHUNK, P]),
                        dst_t[:, ds(c * CHUNK, CHUNK)].rearrange("p (k a) -> p k a", a=1
                                                                 ).to_broadcast([P, CHUNK, P]),
                        ALU.is_equal).then_inc(s_sel, 1)

            def inverse_degree(order, j, b):
                dve.wait_ge(s_acc, j + 1)
                order.then(dve.tensor_scalar_max(rdeg[:, b, 0:1], acc[:, D:D + 1], 1.0))
                dve.reciprocal(rdeg[:, b, 1:2], rdeg[:, b, 0:1]).then_inc(s_rdeg, 1)
                dve.wait_ge(s_rdeg, j + 1)

            def mean_low(j, b):
                dve.wait_ge(s_hhi, j + 1)
                dve.scalar_tensor_tensor(hn[:, D:2 * D], acc[:, 0:D], rdeg[:, b, 1:2], hn[:, 0:D],
                                         ALU.mult, ALU.subtract).then_inc(s_hlo, 1)

            def residual(order, j, b):
                dve.wait_ge(s_proj, j + 1)
                x1 = X[:, ds(j, 1), :].rearrange("p a f -> p (a f)")
                dve.scalar_tensor_tensor(x1, proj[:, 0:D], 1.0 / S_PROD, x1, ALU.mult, ALU.add
                                         ).then_inc(s_pfree, 1)
                dve.wait_ge(s_pfree, j + 2)
                dve.sem_inc(s_passed, 1)
                order.then(dve.bn_stats(stats[:, b, :], x1))
                dve.sem_inc(s_passed, 1)
                order.then(dve.bn_aggr(mv_pair[:, b, :], stats[:, b, :]))

            def normalise(j, to):
                return dve.tensor_scalar(to, X[:, ds(j, 1), :].rearrange("p a f -> p (a f)"),
                                         mv[:, ds(j, 1), 0:1].rearrange("p a f -> p (a f)"),
                                         rstd[:, ds(j, 1)], ALU.subtract, ALU.mult)

            def column_sums(order, p, rows):
                order.then(dve.tensor_copy(mv[:, ds(2 * p, 2), 0:1], mv_pair[:, :, 0:1]))
                inverse_deviation(order, mv_pair[:, :, 1],
                                  rstd[:, ds(2 * p, 2)], 2, S_ROW ** -2, LN_EPS * S_ROW ** -2)
                for b in range(2):
                    order.then(normalise(2 * p + b, row_n[:, :]))
                    r = rows[b]
                    order.then(dve.tensor_tensor(colsum[0:r, :], colsum[0:r, :], row_n[0:r, :], ALU.add))

            def rows_scaled(q, tile):
                for h in range(2):
                    normalise(tile + h, xs[:, h, :]).then_inc(s_x2s, 1)
                for h in range(2):
                    dve.wait_ge(s_x2h, 2 * q + h + 1)
                    dve.tensor_tensor(x2[:, h, D:2 * D], xs[:, h, :], x2[:, h, 0:D], ALU.subtract
                                      ).then_inc(s_x2l, 1)

            def hidden_low(q, g):
                e, b = g // 2, g % 2
                dve.wait_ge(s_gh, 4 * q + g + 1)
                dve.scalar_tensor_tensor(gl[:, e, 2 * b:2 * b + 2, :], g32[:, b, :, :], S_G,
                                         gh[:, e, 2 * b:2 * b + 2, :], ALU.mult, ALU.subtract
                                         ).then_inc(s_gl, 1)

            def combined(q):
                for h in range(2):
                    dve.wait_ge(s_y1c, 2 * q + h + 1)
                    dve.tensor_tensor(y_sb[:, h, 0:D], xs[:, h, :], y_sb[:, h, D:2 * D], ALU.add
                                      ).then_inc(s_yu, 1)
                    dve.wait_ge(s_yu, 2 * q + h + 1)
                    dve.scalar_tensor_tensor(y_sb[:, h, D:2 * D], yp[h][:, 0, :], S_ROW / (S_G * S_W),
                                             y_sb[:, h, D:2 * D], ALU.mult, ALU.subtract).then_inc(s_yc, 1)

            def pair(base, p, q=None, between=None, ahead=False, first=False):
                order = Order(dve, base)
                j = 2 * p
                dve.sem_inc(s_passed, 1)
                window(order, j)
                if not first:
                    residual(order, j - 1, 1)
                    column_sums(order, p - 1, (P, P))
                if between:
                    between(order)
                inverse_degree(order, j, 0)
                mean_low(j, 0)
                if q is not None:
                    hidden_low(q, 0)
                    hidden_low(q, 1)
                dve.sem_inc(s_passed, 1)
                window(order, j + 1)
                residual(order, j, 0)
                if q is not None:
                    hidden_low(q, 2)
                inverse_degree(order, j + 1, 1)
                mean_low(j + 1, 1)
                if q is not None:
                    hidden_low(q, 3)
                    combined(q)
                if ahead:
                    rows_scaled(0 if q is None else q + 1, 0 if q is None else 2 * (q + 1))
                return order.n

            def row(k, n=EXPERTS, at=0):
                return rt[0:1, k, at:at + n]

            def router(order, k, nodes, bank):
                dve.sem_inc(s_gnn, 1)
                dve.wait_ge(s_mean, k + 1)
                dve.tensor_scalar(mean_t[:, :], bank[:, 0:DC], 1.0 / (S_ROW * nodes), None, ALU.mult
                                  ).then_inc(s_meanc, 1)
                dve.wait_ge(s_log, k + 1)
                order.then(dve.tensor_tensor(row(2), bank[0:1, 16:16 + EXPERTS], row(0), ALU.add))

                def negative_max(n, of):
                    order.then(dve.reduce_max(row(n, 1, 2), row(of), AX.X))
                    dve.tensor_scalar(row(n, 1), row(n, 1, 2), -1.0, None, ALU.mult).then_inc(s_nmax, 1)

                negative_max(3, 2)
                dve.wait_ge(s_exp, 2 * k + 1)
                order.then(dve.reciprocal(row(3, 1, 3), row(3, 1, 1)))
                order.then(dve.tensor_scalar(row(4), row(2), row(3, 1, 3), None, ALU.mult))
                order.then(dve.tensor_scalar(row(5), row(4), float(N_NODES), None, ALU.mult))
                order.then(dve.reciprocal(row(9), row(5)))
                order.then(dve.tensor_scalar(row(9), row(9), CAPACITY, 1.0, ALU.mult, ALU.min))
                order.then(dve.tensor_tensor(row(6), row(4), row(9), ALU.mult))
                negative_max(7, 6)
                dve.wait_ge(s_exp, 2 * k + 2)
                order.then(dve.reciprocal(row(7, 1, 3), row(7, 1, 1)))
                order.then(dve.tensor_scalar(row(8), row(6), row(7, 1, 3), None, ALU.mult))
                order.then(dve.tensor_copy(row(18), row(8)))
                for n in range(TOP):
                    order.then(dve.reduce_max(row(12, 1, n), row(18), AX.X))
                    order.then(dve.tensor_scalar(row(13), row(18), row(12, 1, n), 2.0 * EXPERTS,
                                                 ALU.is_lt, ALU.mult))
                    order.then(dve.tensor_tensor(row(13), row(13), iota_e[:, :], ALU.add))
                    order.then(dve.tensor_reduce(row(14, 1, n), row(13), AX.X, ALU.min))
                    if n == 0:
                        order.then(dve.tensor_scalar(row(15), iota_e[:, :], row(14, 1, 0), -2.0,
                                                     ALU.is_equal, ALU.mult))
                        order.then(dve.tensor_tensor(row(18), row(18), row(15), ALU.add))

            def predict(order):
                router(order, 0, 2 * P * PREDICT, yp_flat[0])
                order.then(dve.tensor_copy(row(16, TOP), row(14, TOP)))
                dve.tensor_copy(ri[:, 0, 0:TOP], row(14, TOP)).then_inc(s_ridx, 1)

            def either(order, to, of):
                order.then(dve.tensor_scalar(row(to), iota_e[:, :], row(of, 1, 0), None, ALU.is_equal))
                order.then(dve.scalar_tensor_tensor(row(to), iota_e[:, :], row(of, 1, 1), row(to),
                                                    ALU.is_equal, ALU.add))

            def decide(order):
                router(order, 1, N_NODES, proj)
                either(order, 13, 14)
                either(order, 15, 16)
                order.then(dve.tensor_tensor(row(13), row(13), row(15), ALU.not_equal))
                order.then(dve.reduce_max(row(17, 1, 1), row(13), AX.X))
                order.then(dve.tensor_tensor(row(14, TOP), row(14, TOP), row(16, TOP), ALU.subtract))
                order.then(dve.scalar_tensor_tensor(row(16, TOP), row(14, TOP), row(17, 1, 1),
                                                    row(16, TOP), ALU.mult, ALU.add))
                order.then(dve.tensor_copy(ri[:, 1, 0:TOP], row(16, TOP)))
                dve.tensor_copy(ri[:, 1, TOP:TOP + 1], row(17, 1, 1)).then_inc(s_ridx, 1)
                for n in range(TOP):
                    order.then(dve.scalar_tensor_tensor(row(13), iota_e[:, :], row(16, 1, n), row(8),
                                                        ALU.is_equal, ALU.mult))
                    order.then(dve.reduce_max(row(12, 1, n), row(13), AX.X))
                dve.tensor_tensor(row(10, 1, 1), row(12, 1, 1), row(12, 1, 0), ALU.subtract
                                  ).then_inc(s_nmax, 1)
                dve.wait_ge(s_exp, 5)
                order.then(dve.tensor_scalar(row(10, 1, 3), row(10, 1, 2), 1.0, None, ALU.add))
                dve.reciprocal(row(11, 1), row(10, 1, 3)).then_inc(s_w0, 1)
                dve.wait_ge(s_wb, 1)
                order.then(dve.tensor_copy(wcol[:, :], proj[:, 32:33]))

            def expert_weights(order, k, e):
                at = 2 * TOP * k + 2 * e
                dve.wait_ge(s_wst, 16 * at + 32)
                for c in range(DC):
                    view = w_stage[0][:, c * HID:(c + 1) * HID].rearrange("p (k h) -> p h k", h=HC)
                    order.then(dve.tensor_scalar(w1_s[:, e, 0, c, :, :], view, S_W, None, ALU.mult))
                    low = dve.scalar_tensor_tensor(w1_s[:, e, 1, c, :, :], view, S_W,
                                                   w1_s[:, e, 0, c, :, :], ALU.mult, ALU.subtract)
                    if c == DC - 1:
                        low.then_inc(s_ew, 1)
                view = w_stage[1].rearrange("p (h n) -> p h n", h=HC)
                order.then(dve.tensor_scalar(w2_s[:, e, 0, :, :], view, S_W, None, ALU.mult))
                dve.scalar_tensor_tensor(w2_s[:, e, 1, :, :], view, S_W, w2_s[:, e, 0, :, :],
                                         ALU.mult, ALU.subtract).then_inc(s_ew, 1)
                if e == TOP - 1:
                    dve.wait_ge(s_ebias, 32 * TOP * (k + 1))
                    order.then(dve.tensor_scalar(bias_rows[0:1, 1:3, :], bias_in[0:1, :, :], S_B2, None,
                                                 ALU.mult))
                    dve.scalar_tensor_tensor(bias_lo[0:1, :, :], bias_in[0:1, :, :], S_B2,
                                             bias_rows[0:1, 1:3, :], ALU.mult, ALU.subtract
                                             ).then_inc(s_blo, 1)

            dve.sem_inc(s_gl, 2)
            dve.sem_inc(s_yc, 2)

            PER_PAIR = 2 * 4 + 1 + NEWTON + 4
            done[0] += pair(done[0], 0, first=True)
            base = done[0]
            with dve.Fori(1, PREDICT) as p:
                assert pair(base + (p - 1) * PER_PAIR, p) == PER_PAIR
            done[0] += (PREDICT - 1) * PER_PAIR
            done[0] += pair(done[0], PREDICT, between=predict)
            done[0] += pair(done[0], PREDICT + 1, between=lambda o: expert_weights(o, 0, 0))
            done[0] += pair(done[0], PREDICT + 2, between=lambda o: expert_weights(o, 0, 1), ahead=True)
            base = done[0]
            with dve.Fori(LAG, NPAIR - 1) as p:
                assert pair(base + (p - LAG) * PER_PAIR, p, p - LAG, ahead=True) == PER_PAIR
            done[0] += (NPAIR - 1 - LAG) * PER_PAIR
            done[0] += pair(done[0], NPAIR - 1, NPAIR - 1 - LAG)
            order = Order(dve, done[0])
            residual(order, NT - 1, 1)
            column_sums(order, NPAIR - 1, (P, LAST_ROWS))
            decide(order)

            def experts_only(q, tile):
                rows_scaled(q, tile)
                for g in range(2 * TOP):
                    hidden_low(q, g)
                combined(q)

            with dve.Fori(NPAIR - LAG, NPAIR) as q:
                experts_only(q, 2 * q)
            again = dve.value_load(ri[0:1, 1, TOP:TOP + 1], min_val=0, max_val=1)
            with dve.If(again > 0):
                for e in range(TOP):
                    expert_weights(order, 1, e)
                with dve.Fori(0, NPAIR) as q:
                    experts_only(q + NPAIR, 2 * q)

            order = Order(dve, 0, s_dvf)

            def outputs(g):
                for t in range(FIN_T):
                    j = g * FIN_T + t
                    dve.wait_ge(s_fg, j + 1)
                    dve.wait_ge(s_beta, j + 1)
                    dve.tensor_tensor(fin[:, g % FIN_B, t, 0:D], fin[:, g % FIN_B, t, D:2 * D],
                                      X[:, j, :], ALU.add).then_inc(s_fo, 1)

            for g in range(FIN_G):
                dve.wait_ge(s_fl[g % FIN_B], 16 * (g // FIN_B + 1))
                lo = g * FIN_T
                z = fin[:, g % FIN_B, :, 0:D]
                order.then(dve.scalar_tensor_tensor(z, fin[:, g % FIN_B, :, D:2 * D], wcol[:, :], z,
                                                    ALU.mult, ALU.add))
                for t in range(FIN_T):
                    dve.bn_stats(stats[:, t, :], fin[:, g % FIN_B, t, 0:D]).then_inc(s_dvf, 1)
                order.n += FIN_T
                dve.wait_ge(s_dvf, order.base + order.n)
                for t in range(FIN_T):
                    dve.bn_aggr(mv[:, lo + t, :], stats[:, t, :]).then_inc(s_dvf, 1)
                order.n += FIN_T
                dve.wait_ge(s_dvf, order.base + order.n)
                inverse_deviation(order, mv[:, lo:lo + FIN_T, 1], rstd[:, lo:lo + FIN_T], FIN_T,
                                  1.0, LN_EPS * S_ROW ** 2)
                dve.scalar_tensor_tensor(mv[:, lo:lo + FIN_T, 0], mv[:, lo:lo + FIN_T, 0], -1.0,
                                         rstd[:, lo:lo + FIN_T], ALU.mult, ALU.mult).then_inc(s_fr, 1)
                if g:
                    outputs(g - 1)
            outputs(FIN_G - 1)


INPUTS = ["x", "src", "dst", "L0_gnn_W_neigh", "L0_gnn_W_self", "L0_gnn_b_self", "L0_ffn_Wr", "L0_ffn_br",
          "L0_ffn_W1", "L0_ffn_b1", "L0_ffn_W2", "L0_ffn_b2", "L0_ffn_gamma", "L0_ffn_beta"]


def kernel(**inputs):
    import concourse.bacc as bacc
    from concourse.bass_utils import run_bass_kernel_spmd

    nc = bacc.Bacc("TRN2", target_bir_lowering=False, num_devices=1)
    arrays, args = {}, []
    for name in INPUTS:
        a = np.ascontiguousarray(inputs[name])
        arrays[f"in_{name}"] = a
        args.append(nc.dram_tensor(f"in_{name}", a.shape, mybir.dt.from_np(a.dtype),
                                   kind="ExternalInput").ap())
    args.append(nc.dram_tensor("out_0", (N_NODES, D), mybir.dt.float32, kind="ExternalOutput").ap())
    gnn_ffn(nc, *args)
    r = run_bass_kernel_spmd(nc, [arrays], core_ids=[0])
    return r.results[0]["out_0"]
```
